# Optimizing a Trainium2 kernel written in Bass

```python
import numpy as np
import jax
import jax.numpy as jnp

def _softmax(x, axis=-1):
    return jax.nn.softmax(x, axis=axis)

def _gelu(x):
    return jax.nn.gelu(x, approximate=True)

def _silu(x):
    return jax.nn.silu(x)

def _sigmoid(x):
    return jax.nn.sigmoid(x)

def _layernorm(x, axis=-1, eps=1e-05):
    m = jnp.mean(x, axis=axis, keepdims=True)
    v = jnp.var(x, axis=axis, keepdims=True)
    return (x - m) / jnp.sqrt(v + eps)

def _scatter_add(tgt, idx, src, axis=0):
    return tgt.at[idx].add(src)

def _segment_sum(src, seg, n):
    return jax.ops.segment_sum(src, seg, n)
kernel_name = 'mk_conv_seq_d2_conv_nchw128_r4_f4dc82'

def setup_inputs(seed: int=0):
    np.random.seed(seed)
    _w = jnp.asarray

    def _rec_inputs():
        import jax
        import jax.numpy as jnp
        _gk = jax.random.key(seed)
        x = -0.0003929 + 0.9999 * jax.random.normal(jax.random.fold_in(_gk, 1), (32, 32, 16, 16), jnp.float32)
        return x
    x = _rec_inputs()

    def _L0_conv_setup():
        import jax, jax.numpy as jnp
        import numpy as np
        from jax import lax
        DIM = 32
        HEADS = 4
        MLP_RATIO = 4
        EPS = 1e-05

        def _conv(x, w, b, groups=1, pad=0):
            y = lax.conv_general_dilated(x, w, window_strides=(1, 1), padding=[(pad, pad), (pad, pad)], feature_group_count=groups, dimension_numbers=('NCHW', 'OIHW', 'NCHW'))
            return y + b[None, :, None, None]

        def _avg_pool_3s2p1(x):
            s = lax.reduce_window(x, 0.0, lax.add, (1, 1, 3, 3), (1, 1, 2, 2), [(0, 0), (0, 0), (1, 1), (1, 1)])
            return s / 9.0

        def _max_pool_2s2(x):
            return lax.reduce_window(x, -jnp.inf, lax.max, (1, 1, 2, 2), (1, 1, 2, 2), [(0, 0), (0, 0), (0, 0), (0, 0)])

        def _biasfree_ln(x, w):
            mu = jnp.mean(x, axis=1, keepdims=True)
            var = jnp.mean((x - mu) ** 2, axis=1, keepdims=True)
            return x / jnp.sqrt(var + EPS) * w[None, :, None, None]

        def _gelu(x):
            return jax.nn.gelu(x, approximate=False)

        def _elgca_attn(x, dw_w, dw_b, qkvl_w, qkvl_b):
            B, C, H, W = x.shape
            C2, C4 = (C // 2, C // 4)
            x1, x2 = (x[:, :C2], x[:, C2:])
            x1 = _gelu(_conv(x1, dw_w, dw_b, groups=C2, pad=1))
            x2 = _gelu(_conv(x2, qkvl_w, qkvl_b))
            x2 = x2.reshape(B, HEADS, C4, H, W)
            q = jnp.sum(x2[:, :HEADS - 3], axis=1)
            k = x2[:, HEADS - 3]
            v = x2[:, HEADS - 2].reshape(B, C4, H * W)
            lfeat = x2[:, HEADS - 1]
            qf = _avg_pool_3s2p1(q).reshape(B, C4, -1)
            kf = _max_pool_2s2(k).reshape(B, C4, -1)
            qk = jnp.einsum('bcn,bdn->bcd', qf, kf)
            attn = jnp.swapaxes(jax.nn.softmax(qk, axis=1), 1, 2)
            out = jnp.einsum('bcd,bdn->bcn', attn, v).reshape(B, C4, H, W)
            return jnp.concatenate([x1, lfeat, out], axis=1)

        def _elgca_mlp(x, fc1_w, fc1_b, pos_w, pos_b, fc2_w, fc2_b):
            h = _gelu(_conv(x, fc1_w, fc1_b))
            h = h + _gelu(_conv(h, pos_w, pos_b, groups=h.shape[1], pad=1))
            return _conv(h, fc2_w, fc2_b)
        key = jax.random.key(seed)
        ks = jax.random.split(key, 10)
        C = DIM
        C2, C4, CH = (C // 2, C // 4, C * MLP_RATIO)
        s = 0.05
        return {'x': jax.random.normal(ks[0], (32, C, 16, 16), dtype=jnp.float32), 'ln1_w': jnp.ones((C,), jnp.float32), 'ln2_w': jnp.ones((C,), jnp.float32), 'dw_w': jax.random.normal(ks[1], (C2, 1, 3, 3), jnp.float32) * s, 'dw_b': jnp.zeros((C2,), jnp.float32), 'qkvl_w': jax.random.normal(ks[2], (C4 * HEADS, C2, 1, 1), jnp.float32) * s, 'qkvl_b': jnp.zeros((C4 * HEADS,), jnp.float32), 'fc1_w': jax.random.normal(ks[3], (CH, C, 1, 1), jnp.float32) * s, 'fc1_b': jnp.zeros((CH,), jnp.float32), 'pos_w': jax.random.normal(ks[4], (CH, 1, 3, 3), jnp.float32) * s, 'pos_b': jnp.zeros((CH,), jnp.float32), 'fc2_w': jax.random.normal(ks[5], (C, CH, 1, 1), jnp.float32) * s, 'fc2_b': jnp.zeros((C,), jnp.float32)}
    _L0_conv_all = _L0_conv_setup()
    _L0_conv_in = {k: v for k, v in _L0_conv_all.items() if k in ('ln1_w', 'ln2_w', 'dw_w', 'dw_b', 'qkvl_w', 'qkvl_b', 'fc1_w', 'fc1_b', 'pos_w', 'pos_b', 'fc2_w', 'fc2_b')}
    del _L0_conv_all

    def _L1_conv_setup():
        import jax, jax.numpy as jnp
        import numpy as np
        B, C, H, W = (4, 32, 16, 16)
        key = jax.random.key(seed)
        ks = jax.random.split(key, 4)
        X = jax.random.normal(ks[0], (B, C, H, W), dtype=jnp.float32)
        Wq = jax.random.normal(ks[1], (C, C), dtype=jnp.float32) * 0.05
        Wk = jax.random.normal(ks[2], (C, C), dtype=jnp.float32) * 0.05
        Wv = jax.random.normal(ks[3], (C, C), dtype=jnp.float32) * 0.05
        bq = jnp.zeros((C,), dtype=jnp.float32)
        bk = jnp.zeros((C,), dtype=jnp.float32)
        bv = jnp.zeros((C,), dtype=jnp.float32)
        return {'X': X, 'Wq': Wq, 'bq': bq, 'Wk': Wk, 'bk': bk, 'Wv': Wv, 'bv': bv}
    _L1_conv_all = _L1_conv_setup()
    _L1_conv_in = {k: v for k, v in _L1_conv_all.items() if k in ('Wq', 'bq', 'Wk', 'bk', 'Wv', 'bv')}
    del _L1_conv_all
    return {'x': x, 'L0_conv_ln1_w': _L0_conv_in['ln1_w'], 'L0_conv_ln2_w': _L0_conv_in['ln2_w'], 'L0_conv_dw_w': _L0_conv_in['dw_w'], 'L0_conv_dw_b': _L0_conv_in['dw_b'], 'L0_conv_qkvl_w': _L0_conv_in['qkvl_w'], 'L0_conv_qkvl_b': _L0_conv_in['qkvl_b'], 'L0_conv_fc1_w': _L0_conv_in['fc1_w'], 'L0_conv_fc1_b': _L0_conv_in['fc1_b'], 'L0_conv_pos_w': _L0_conv_in['pos_w'], 'L0_conv_pos_b': _L0_conv_in['pos_b'], 'L0_conv_fc2_w': _L0_conv_in['fc2_w'], 'L0_conv_fc2_b': _L0_conv_in['fc2_b'], 'L1_conv_Wq': _L1_conv_in['Wq'], 'L1_conv_bq': _L1_conv_in['bq'], 'L1_conv_Wk': _L1_conv_in['Wk'], 'L1_conv_bk': _L1_conv_in['bk'], 'L1_conv_Wv': _L1_conv_in['Wv'], 'L1_conv_bv': _L1_conv_in['bv']}

def reference(x, L0_conv_ln1_w, L0_conv_ln2_w, L0_conv_dw_w, L0_conv_dw_b, L0_conv_qkvl_w, L0_conv_qkvl_b, L0_conv_fc1_w, L0_conv_fc1_b, L0_conv_pos_w, L0_conv_pos_b, L0_conv_fc2_w, L0_conv_fc2_b, L1_conv_Wq, L1_conv_bq, L1_conv_Wk, L1_conv_bk, L1_conv_Wv, L1_conv_bv):
    import jax
    import jax.numpy as jnp

    def _L0_conv_ref(x, ln1_w, ln2_w, dw_w, dw_b, qkvl_w, qkvl_b, fc1_w, fc1_b, pos_w, pos_b, fc2_w, fc2_b):
        import jax, jax.numpy as jnp
        import numpy as np
        from jax import lax
        DIM = 32
        HEADS = 4
        MLP_RATIO = 4
        EPS = 1e-05

        def _conv(x, w, b, groups=1, pad=0):
            y = lax.conv_general_dilated(x, w, window_strides=(1, 1), padding=[(pad, pad), (pad, pad)], feature_group_count=groups, dimension_numbers=('NCHW', 'OIHW', 'NCHW'))
            return y + b[None, :, None, None]

        def _avg_pool_3s2p1(x):
            s = lax.reduce_window(x, 0.0, lax.add, (1, 1, 3, 3), (1, 1, 2, 2), [(0, 0), (0, 0), (1, 1), (1, 1)])
            return s / 9.0

        def _max_pool_2s2(x):
            return lax.reduce_window(x, -jnp.inf, lax.max, (1, 1, 2, 2), (1, 1, 2, 2), [(0, 0), (0, 0), (0, 0), (0, 0)])

        def _biasfree_ln(x, w):
            mu = jnp.mean(x, axis=1, keepdims=True)
            var = jnp.mean((x - mu) ** 2, axis=1, keepdims=True)
            return x / jnp.sqrt(var + EPS) * w[None, :, None, None]

        def _gelu(x):
            return jax.nn.gelu(x, approximate=False)

        def _elgca_attn(x, dw_w, dw_b, qkvl_w, qkvl_b):
            B, C, H, W = x.shape
            C2, C4 = (C // 2, C // 4)
            x1, x2 = (x[:, :C2], x[:, C2:])
            x1 = _gelu(_conv(x1, dw_w, dw_b, groups=C2, pad=1))
            x2 = _gelu(_conv(x2, qkvl_w, qkvl_b))
            x2 = x2.reshape(B, HEADS, C4, H, W)
            q = jnp.sum(x2[:, :HEADS - 3], axis=1)
            k = x2[:, HEADS - 3]
            v = x2[:, HEADS - 2].reshape(B, C4, H * W)
            lfeat = x2[:, HEADS - 1]
            qf = _avg_pool_3s2p1(q).reshape(B, C4, -1)
            kf = _max_pool_2s2(k).reshape(B, C4, -1)
            qk = jnp.einsum('bcn,bdn->bcd', qf, kf)
            attn = jnp.swapaxes(jax.nn.softmax(qk, axis=1), 1, 2)
            out = jnp.einsum('bcd,bdn->bcn', attn, v).reshape(B, C4, H, W)
            return jnp.concatenate([x1, lfeat, out], axis=1)

        def _elgca_mlp(x, fc1_w, fc1_b, pos_w, pos_b, fc2_w, fc2_b):
            h = _gelu(_conv(x, fc1_w, fc1_b))
            h = h + _gelu(_conv(h, pos_w, pos_b, groups=h.shape[1], pad=1))
            return _conv(h, fc2_w, fc2_b)
        h = _biasfree_ln(x, ln1_w)
        h = _elgca_attn(h, dw_w, dw_b, qkvl_w, qkvl_b)
        out = h + x
        m = _biasfree_ln(out, ln2_w)
        m = _elgca_mlp(m, fc1_w, fc1_b, pos_w, pos_b, fc2_w, fc2_b)
        return out + m

    def _L1_conv_ref(X, Wq, bq, Wk, bk, Wv, bv):
        import jax, jax.numpy as jnp
        import numpy as np
        B, C, H, W = (4, 32, 16, 16)
        b, c, h, w = X.shape
        hw = h * w

        def proj(Wm, bias):
            y = jnp.einsum('bchw,oc->bohw', X, Wm) + bias[None, :, None, None]
            return y.reshape(b, c, hw).transpose(0, 2, 1)
        q = proj(Wq, bq)
        k = proj(Wk, bk)
        v = proj(Wv, bv)
        scores = jnp.einsum('bic,bjc->bij', q, k)
        a = jax.nn.softmax(scores, axis=1)
        x = jnp.einsum('bij,bjc->bic', a, v)
        x = x.transpose(0, 2, 1).reshape(b, c, h, w)
        return X + x

    def _gn(v, G=32, eps=1e-05):
        B_, C_, H_, W_ = v.shape
        g = v.reshape(B_, G, C_ // G, H_, W_)
        m = jnp.mean(g, axis=(2, 3, 4), keepdims=True)
        s = jnp.var(g, axis=(2, 3, 4), keepdims=True)
        return ((g - m) / jnp.sqrt(s + eps)).reshape(v.shape)

    def _ln_c(v, eps=1e-06):
        m = jnp.mean(v, axis=1, keepdims=True)
        s = jnp.var(v, axis=1, keepdims=True)
        return (v - m) / jnp.sqrt(s + eps)

    def _ln_t(v, eps=1e-05):
        m = jnp.mean(v, axis=-1, keepdims=True)
        s = jnp.var(v, axis=-1, keepdims=True)
        return (v - m) / jnp.sqrt(s + eps)

    def _to_tokens(v):
        B_, C_, H_, W_ = v.shape
        return v.reshape(B_, C_, H_ * W_).transpose(0, 2, 1)

    def _from_tokens(t, like):
        B_, C_, H_, W_ = like.shape
        return t.transpose(0, 2, 1).reshape(B_, C_, H_, W_)
    x = _L0_conv_ref(x, L0_conv_ln1_w, L0_conv_ln2_w, L0_conv_dw_w, L0_conv_dw_b, L0_conv_qkvl_w, L0_conv_qkvl_b, L0_conv_fc1_w, L0_conv_fc1_b, L0_conv_pos_w, L0_conv_pos_b, L0_conv_fc2_w, L0_conv_fc2_b)
    x = _L1_conv_ref(x, L1_conv_Wq, L1_conv_bq, L1_conv_Wk, L1_conv_bk, L1_conv_Wv, L1_conv_bv)
    return x

_drawn_inputs = setup_inputs


def setup_inputs(seed=0):
    import zlib

    import numpy as np

    out = dict(_drawn_inputs(seed))
    spreads = {'L0_conv_ln1_w': (1.0, 0.6),
     'L0_conv_ln2_w': (1.0, 0.6),
     'L0_conv_dw_b': (0.0, 0.1),
     'L0_conv_qkvl_b': (0.0, 0.407),
     'L0_conv_fc1_b': (0.0, 0.1),
     'L0_conv_pos_b': (0.0, 0.1),
     'L0_conv_fc2_b': (0.0, 0.1),
     'L1_conv_bq': (0.0, 0.8),
     'L1_conv_bk': (0.0, 0.427),
     'L1_conv_bv': (0.0, 0.1)}
    factors = {'L0_conv_pos_w': 8.0}
    for name, (base, spread) in spreads.items():
        noise = np.random.default_rng([zlib.crc32(name.encode()), seed]).standard_normal(out[name].shape)
        drawn = base * np.exp(spread * noise) if base else spread * noise
        out[name] = jnp.asarray(drawn.astype(out[name].dtype))
    for name, factor in factors.items():
        out[name] = (out[name] * factor).astype(out[name].dtype)
    return out
```

```python
from contextlib import ExitStack

import concourse.bass as bass
from concourse import mybir

ALU = mybir.AluOpType
ACT = mybir.ActivationFunctionType
F32 = mybir.dt.float32
AX_X = mybir.AxisListType.X

P = 128
C = 32
G = P // C
B = 32
SIDE = 16
NPIX = SIDE * SIDE
HALVES = 2
BH = B // G // HALVES
COLS = BH * NPIX
BANK = 512
NB = COLS // BANK
C2, C4 = C // 2, C // 4
HID = 128
ROW = SIDE + 1
PROWS = (SIDE + 2) * BH + 1
PADDED = PROWS * ROW
INNER = BH * ROW + 1
ROWS = SIDE * BH
TOK = COLS // P
PAIRS = BH // 2
CLASSES = 4
POOLED = NPIX // 4
BATCH_ORDER = [0, 2, 1, 3]
LN_EPS = 1e-5

TAPS = [(dy, dx) for dy in (-1, 0, 1) for dx in (-1, 0, 1)]
CENTRE = 4
ATTN_PE_TAPS = [4, 0, 1, 2]
ATTN_DVE_TAPS = [t for t in range(9) if t not in ATTN_PE_TAPS]
MLP_PE_TAPS = [0, 1, 2]
MLP_DVE_TAPS = [t for t in range(9) if t not in MLP_PE_TAPS]


def columns(sizes):
    at, out = 0, {}
    for name, n in sizes:
        out[name] = (at, at + n)
        at += n
    return out, at


FIRST_COLS, FIRST_N = columns([("centre", P), ("ident", P), ("mean", G), ("ln1_w", 1), ("ln2_w", 1)])
SECOND_COLS, SECOND_N = columns([
    ("attn_taps", P * len(ATTN_PE_TAPS)), ("attn_w", 9), ("attn_b", 1), ("qk_w", 2 * G * C4),
    ("qk_brow", 2 * G * C4), ("ones", P), ("pool", CLASSES * P), ("keep", P), ("is_v", 1),
])
THIRD_COLS, THIRD_N = columns([
    ("fc1_w", 2 * HID), ("fc1_b", 1), ("mlp_taps", P * len(MLP_PE_TAPS)), ("pos_w", 9), ("pos_b", 1),
    ("fc2_w", C), ("fc2_b", 1), ("wq", P), ("wk", P), ("wv", P), ("bq", 1), ("bk", 1), ("bv", P),
    ("minus_even", 1), ("minus_odd", 1),
])


def build(nc, x_in, first_in, second_in, third_in, out):
    with ExitStack() as ctx:
        def sb(name, shape):
            return ctx.enter_context(nc.sbuf_tensor(name, shape, F32))

        def sem(name):
            return ctx.enter_context(nc.semaphore(name))

        ps = ctx.enter_context(nc.psum_tensor("ps", [P, 8, BANK], F32))

        x = sb("x", [P, HALVES, COLS])
        first = sb("first", [P, FIRST_N])
        second = sb("second", [P, SECOND_N])
        third = sb("third", [P, THIRD_N])
        padded = sb("padded", [P, HALVES * (1 + G), PADDED])
        acc = sb("acc", [P, HALVES * G, COLS])
        var_tok = sb("var_tok", [P, 2, HALVES, TOK * G])
        rstd_tok = sb("rstd_tok", [P, 2, HALVES, TOK * G])
        norm_parity = acc[:, 4:6, :].rearrange("p h (k n) -> p h k n", k=CLASSES)
        rstd_wide = acc[:, 6:8, :]
        eps_col = sb("eps_col", [P, 1])
        qk_tok = sb("qk_tok", [P, HALVES, PAIRS * CLASSES * 2 * G * C4])
        kf = sb("kf", [P, HALVES, PAIRS, P])
        qf = sb("qf", [P, HALVES, PAIRS, G * C4])
        att = sb("att", [P, HALVES, BH, C4])
        att_max = sb("att_max", [P, HALVES, BH])
        att_sum = sb("att_sum", [P, HALVES, BH])
        att_inv = sb("att_inv", [P, HALVES, BH])
        att_blocks = sb("att_blocks", [P, HALVES, BH, P])
        mix_w = sb("mix_w", [P, HALVES, BH, P])
        res1 = sb("res1", [P, HALVES, COLS])
        skip = sb("skip", [P, HALVES, COLS])
        m = sb("m", [P, HALVES, COLS])
        X = sb("X", [P, HALVES, COLS])
        k_split = sb("k_split", [P, 2, HALVES, COLS])
        v_tok = sb("v_tok", [P, HALVES * BH, 2, G, C])
        prob = sb("prob", [P, 2, G, 2, NPIX])
        smin = sb("smin", [P, HALVES * BH * 2, 4])
        psum_row = sb("psum_row", [P, HALVES * BH, 2, G])
        inv_row = sb("inv_row", [P, HALVES * BH, 2, G])
        y_out = sb("y_out", [P, HALVES * BH, NPIX])

        def c1(name):
            return first[:, FIRST_COLS[name][0]:FIRST_COLS[name][1]]

        def c2(name):
            return second[:, SECOND_COLS[name][0]:SECOND_COLS[name][1]]

        def c3(name):
            return third[:, THIRD_COLS[name][0]:THIRD_COLS[name][1]]

        def big(H, n=NB):
            return ps[:, 4 * H:4 * H + n, :]

        def small(H, which):
            return ps[:, 4 * H + NB + which, :]

        def tap_view(buf, tap, bank=None):
            dy, dx = TAPS[tap]
            off = INNER + dy * BH * ROW + dx
            n = ROWS if bank is None else ROWS // NB
            off += 0 if bank is None else bank * n * ROW
            return padded[:, buf, off:off + n * ROW].rearrange("p (r s) -> p r s", s=ROW)[:, :, 0:SIDE]

        def rows(ap):
            return ap.rearrange("p (r s) -> p r s", s=SIDE)

        def by_batch(ap):
            return ap.rearrange("p (y b s) -> p b y s", b=BH, s=SIDE)

        x_loaded = [sem(f"x_loaded{H}") for H in range(HALVES)]
        first_loaded, second_loaded, third_loaded = sem("first_loaded"), sem("second_loaded"), sem("third_loaded")
        dve_zeroed, pool_zeroed = sem("dve_zeroed"), sem("pool_zeroed")
        parity_split, skip_ready = sem("parity_split"), sem("skip_ready")
        centred, squared, var_ready = sem("centred"), sem("squared"), sem("var_ready")
        std_ready, rstd_ready, rstd_spread, normed = (
            sem("std_ready"), sem("rstd_ready"), sem("rstd_spread"), sem("normed"))
        attn_conv_pe, qk_proj, qk_gelu, k_pooled = (
            sem("attn_conv_pe"), sem("qk_proj"), sem("qk_gelu"), sem("k_pooled"))
        q_pooled, q_scaled, att_scores, att_exp_in, att_exp = (
            sem("q_pooled"), sem("q_scaled"), sem("att_scores"), sem("att_exp_in"), sem("att_exp"))
        att_placed, att_turned, mix_ready, attn_conv, attn_gelu, mixed, res1_ready = (
            sem("att_placed"), sem("att_turned"), sem("mix_ready"), sem("attn_conv"), sem("attn_gelu"),
            sem("mixed"), sem("res1_ready"))
        fc1_done, hid_gelu, conv_pe, conv_read, conv_done, conv_gelu, fc2_done, X_ready = (
            sem("fc1_done"), sem("hid_gelu"), sem("conv_pe"), sem("conv_read"), sem("conv_done"),
            sem("conv_gelu"), sem("fc2_done"), sem("X_ready"))
        q_proj, q_ready, k_proj, k_ready, v_proj, v_ready = (
            sem("q_proj"), sem("q_ready"), sem("k_proj"), sem("k_ready"), sem("v_proj"), sem("v_ready"))
        scores_done, max_ready, exp_done, v_scaled, av_done, y_ready, stored = (
            sem("scores_done"), sem("max_ready"), sem("exp_done"), sem("v_scaled"), sem("av_done"),
            sem("y_ready"), sem("stored"))
        dve_chain = sem("dve_chain")

        block = ctx.enter_context(nc.Block())

        @block.sync
        def _(sp):
            sp.dma_start(first[:, :], first_in).then_inc(first_loaded, 16)
            for H in range(HALVES):
                sp.dma_start(x[:, H, :], x_in[:, H * COLS:(H + 1) * COLS]).then_inc(x_loaded[H], 16)
            sp.dma_start(second[:, :], second_in).then_inc(second_loaded, 16)
            sp.dma_start(third[:, :], third_in).then_inc(third_loaded, 16)
            for beta in range(HALVES * BH):
                sp.wait_ge(y_ready, beta + 1)
                sp.dma_start(out[:, beta * NPIX:(beta + 1) * NPIX], y_out[:, beta, :]).then_inc(stored, 16)
            sp.wait_ge(stored, 16 * HALVES * BH)

        @block.gpsimd
        def _(pool):
            pool.memset(kf[:, :, :, :], 0.0).then_inc(pool_zeroed, 1)
            pool.memset(att_blocks[:, :, :, :], 0.0).then_inc(pool_zeroed, 1)
            pool.wait_ge(third_loaded, 16)
            for H in range(HALVES):
                pool.wait_ge(res1_ready, H + 1)
                pool.tensor_scalar(skip[:, H, :].rearrange("p (b y s) -> p b y s", b=BH, s=SIDE),
                                   by_batch(res1[:, H, :]), c3("fc2_b"), None, ALU.add).then_inc(skip_ready, 1)

        @block.tensor
        def _(pe):
            def centre(ln, H, src):
                for n in range(NB):
                    last = pe.matmul(big(H)[:, n, :], c1("centre"), src[:, H, n * BANK:(n + 1) * BANK],
                                     start=True, stop=True)
                last.then_inc(centred, 1)

            def variance(ln, H):
                pe.wait_ge(squared, HALVES * ln + H + 1)
                for t in range(TOK):
                    last = pe.matmul(small(H, 1)[:, t * G:(t + 1) * G], acc[:, 2 + H, t * P:(t + 1) * P],
                                     c1("mean"), start=True, stop=True)
                last.then_inc(var_ready, 1)

            def spread(ln, H):
                pe.wait_ge(rstd_ready, HALVES * ln + H + 1)
                for t in range(TOK):
                    last = pe.matmul(big(H)[:, t * P // BANK, t * P % BANK:t * P % BANK + P],
                                     rstd_wide[:, H, t * P:(t + 1) * P], c1("ident"),
                                     start=True, stop=True)
                last.then_inc(rstd_spread, 1)

            pe.wait_ge(first_loaded, 16)
            for H in range(HALVES):
                pe.wait_ge(x_loaded[H], 16)
                centre(0, H, x)
            for H in range(HALVES):
                variance(0, H)
            for H in range(HALVES):
                spread(0, H)

            pe.wait_ge(second_loaded, 16)
            pe.wait_ge(dve_zeroed, 4)
            for H in range(HALVES):
                pe.wait_ge(parity_split, H + 1)
                pe.matmul(small(H, 0), c2("ones")[0:1, :],
                          c2("qk_brow")[0:1, :].unsqueeze(1).to_broadcast([1, PAIRS * CLASSES, 2 * G * C4]),
                          start=True, stop=False)
                for pair in range(PAIRS):
                    for cl in range(CLASSES):
                        at = (pair * CLASSES + cl) * 2 * G * C4
                        last = pe.matmul(small(H, 0)[:, at:at + 2 * G * C4],
                                         norm_parity[:, H, cl, pair * P:(pair + 1) * P],
                                         c2("qk_w"), start=False, stop=(pair, cl) == (PAIRS - 1, CLASSES - 1))
                last.then_inc(qk_proj, 1)
                pe.wait_ge(normed, H + 1)
                for n in range(NB):
                    for i, tap in enumerate(ATTN_PE_TAPS):
                        last = pe.matmul(big(H)[:, n, :], c2("attn_taps")[:, i * P:(i + 1) * P],
                                         tap_view(H, tap, n), start=i == 0, stop=i == len(ATTN_PE_TAPS) - 1)
                last.then_inc(attn_conv_pe, 1)
            pe.wait_ge(pool_zeroed, 2)
            for H in range(HALVES):
                pe.wait_ge(qk_gelu, H + 1)
                q_cols = qk_tok[:, H, :].rearrange("p (a k w d) -> p a k w d", a=PAIRS, k=CLASSES, w=2)
                for cl in range(CLASSES):
                    last = pe.matmul(small(H, 1)[:, 64:64 + PAIRS * G * C4], c2("pool")[:, cl * P:(cl + 1) * P],
                                     q_cols[:, :, cl, 0, :], start=cl == 0, stop=cl == CLASSES - 1)
                last.then_inc(q_pooled, 1)
            for H in range(HALVES):
                pe.wait_ge(k_pooled, H + 1)
                pe.wait_ge(q_scaled, H + 1)
                for b in BATCH_ORDER:
                    pair, half = b // 2, b % 2
                    lo = POOLED * half
                    last = pe.matmul(small(H, half)[:, 128 + pair * G * C4:128 + (pair + 1) * G * C4],
                                     kf[lo:lo + POOLED, H, pair, :], qf[lo:lo + POOLED, H, pair, :],
                                     start=True, stop=True)
                last.then_inc(att_scores, 1)
            for H in range(HALVES):
                pe.wait_ge(att_placed, H + 1)
                for b in range(BH):
                    last = pe.transpose(small(H, 0)[:, b * P:(b + 1) * P], att_blocks[:, H, b, :], c1("ident"))
                last.then_inc(att_turned, 1)
            for H in range(HALVES):
                pe.wait_ge(mix_ready, H + 1)
                pe.wait_ge(attn_gelu, H + 1)
                for s, b in enumerate(BATCH_ORDER):
                    at = b * NPIX
                    last = pe.matmul(big(H)[:, at // BANK, at % BANK:at % BANK + NPIX], mix_w[:, H, s, :],
                                     by_batch(acc[:, H, :])[:, b, :, :], start=True, stop=True)
                last.then_inc(mixed, 1)
            for H in range(HALVES):
                pe.wait_ge(res1_ready, H + 1)
                centre(1, H, res1)
            for H in range(HALVES):
                variance(1, H)
            for H in range(HALVES):
                spread(1, H)

            pe.wait_ge(third_loaded, 16)
            TILES = HALVES * G

            def fc1(i):
                H, g = i // G, i % G
                pe.wait_ge(normed, HALVES + H + 1)
                if i >= 1:
                    pe.wait_ge(hid_gelu, i)
                lo = 64 * (g // 2)
                w = c3("fc1_w")[lo:lo + 64, (g % 2) * HID:(g % 2 + 1) * HID]
                for n in range(NB):
                    last = pe.matmul(ps[:, n, :], w, m[lo:lo + 64, H, n * BANK:(n + 1) * BANK],
                                     start=True, stop=True)
                last.then_inc(fc1_done, 1)

            def conv(i):
                pe.wait_ge(hid_gelu, i + 1)
                if i == 0:
                    pe.wait_ge(normed, 2 * HALVES)
                if i >= 2:
                    pe.wait_ge(conv_read, i - 1)
                for n in range(NB):
                    for j, tap in enumerate(MLP_PE_TAPS):
                        last = pe.matmul(ps[:, 2 + 2 * (i % 2) + n, :], c3("mlp_taps")[:, j * P:(j + 1) * P],
                                         tap_view(HALVES + i, tap, n), start=j == 0,
                                         stop=j == len(MLP_PE_TAPS) - 1)
                last.then_inc(conv_pe, 1)

            def fc2(H):
                pe.wait_ge(conv_gelu, G * (H + 1))
                if H:
                    pe.wait_ge(X_ready, H)
                for n in range(NB):
                    for part in range(2):
                        for g in range(G):
                            i = G * H + g
                            h = padded[:, HALVES + i, INNER:INNER + ROWS * ROW].rearrange(
                                "p (y b s) -> p b y s", b=BH, s=ROW)[:, :, :, 0:SIDE]
                            rhs = (h, by_batch(acc[:, i, :]))[part][:, 2 * n:2 * n + 2, :, :]
                            last = pe.matmul(ps[C * g:C * (g + 1), 6 + n, :], c3("fc2_w"), rhs,
                                             start=part == 0, stop=part == 1)
                last.then_inc(fc2_done, 1)

            fc1(0)
            fc1(1)
            for pair in range(TILES // 2):
                if pair == 3:
                    fc2(0)
                conv(2 * pair)
                conv(2 * pair + 1)
                if 2 * pair + 2 < TILES:
                    fc1(2 * pair + 2)
                    fc1(2 * pair + 3)
            fc2(1)

            def channel_proj(name, done, H, bank):
                for n in range(NB):
                    last = pe.matmul(ps[:, bank + n, :], c3(name), X[:, H, n * BANK:(n + 1) * BANK],
                                     start=True, stop=True)
                last.then_inc(done, 1)

            def value_proj(H, bank):
                for b in range(BH):
                    for jt in range(2):
                        at = (2 * b + jt) * P
                        last = pe.matmul(ps[:, bank + at // BANK, at % BANK:at % BANK + P],
                                         X[:, H, at:at + P], c3("wv"),
                                         start=True, stop=True)
                last.then_inc(v_proj, 1)

            def scores(n):
                H, b, gp = n // (2 * BH), n // 2 % BH, n % 2
                if n >= 2:
                    pe.wait_ge(exp_done, n - 1)
                for j in range(2):
                    lo = 64 * gp
                    for jt in range(2):
                        at = b * NPIX + jt * P
                        k = k_split[lo:lo + 64, j, H, at:at + P]
                        q = m[lo:lo + 64, H, b * NPIX:(b + 1) * NPIX]
                        last = pe.matmul(ps[:, 2 + 2 * (n % 2) + j, jt * NPIX:(jt + 1) * NPIX], k, q,
                                         start=True, stop=True)
                last.then_inc(scores_done, 1)

            def weighted_values(beta):
                pe.wait_ge(v_scaled, beta + 1)
                if beta >= 2:
                    pe.wait_ge(y_ready, beta - 1)
                for jt in range(2):
                    for g in range(G):
                        last = pe.matmul(ps[C * g:C * (g + 1), 6 + beta % 2, 0:NPIX], v_tok[:, beta, jt, g, :],
                                         prob[:, beta % 2, g, jt, :], start=jt == 0, stop=jt == 1)
                last.then_inc(av_done, 1)

            for H in range(HALVES):
                pe.wait_ge(X_ready, HALVES)
                if H:
                    pe.wait_ge(q_ready, 1)
                channel_proj("wq", q_proj, H, 0)
                if H == 0:
                    channel_proj("wk", k_proj, H, 2)
                    value_proj(H, 4)
                else:
                    pe.wait_ge(q_ready, 2)
                    channel_proj("wk", k_proj, H, 0)
                    pe.wait_ge(k_ready, 2)
                    value_proj(H, 0)
                pe.wait_ge(q_ready, H + 1)
                pe.wait_ge(k_ready, H + 1)
                pe.wait_ge(v_ready, H + 1)
                first_n = H * 2 * BH
                scores(first_n)
                scores(first_n + 1)
                for b in range(BH):
                    beta = H * BH + b
                    if b + 1 < BH:
                        scores(2 * beta + 2)
                        scores(2 * beta + 3)
                    weighted_values(beta)

        @block.scalar
        def _(act):
            def square(ln, H):
                act.wait_ge(centred, HALVES * ln + H + 1)
                act.activation(acc[:, 2 + H, :], big(H).rearrange("p n c -> p (n c)"),
                               ACT.Square).then_inc(squared, 1)

            def root(ln, H):
                act.wait_ge(var_ready, HALVES * ln + H + 1)
                act.activation(var_tok[:, ln, H, :], small(H, 1)[:, 0:TOK * G], ACT.Sqrt,
                               bias=eps_col[:, :]).then_inc(std_ready, 1)

            act.wait_ge(dve_zeroed, 4)
            for H in range(HALVES):
                square(0, H)
            for H in range(HALVES):
                root(0, H)
            for H in range(HALVES):
                act.wait_ge(normed, H + 1)
                whole = padded[:, H, INNER:INNER + ROWS * ROW].rearrange("p (y b s) -> p b y s", b=BH, s=ROW)
                for cl in range(CLASSES):
                    last = act.activation(
                        norm_parity[:, H, cl, :].rearrange("p (b i j) -> p b i j", b=BH, j=SIDE // 2),
                        whole[:, :, cl // 2::2, cl % 2:SIDE:2], ACT.Copy)
                last.then_inc(parity_split, 1)
            act.wait_ge(second_loaded, 16)
            for H in range(HALVES):
                act.wait_ge(qk_proj, H + 1)
                act.activation(qk_tok[:, H, :], small(H, 0), ACT.Gelu).then_inc(qk_gelu, 1)
            for H in range(HALVES):
                act.wait_ge(q_pooled, H + 1)
                act.activation(qf[:, H, :, :].rearrange("p a d -> p (a d)"),
                               small(H, 1)[:, 64:64 + PAIRS * G * C4], ACT.Copy, scale=1.0 / 9.0
                               ).then_inc(q_scaled, 1)
            for H in range(HALVES):
                act.wait_ge(attn_conv, H + 1)
                act.activation(acc[:, H, :], acc[:, H, :], ACT.Gelu, bias=c2("attn_b")).then_inc(attn_gelu, 1)
            for H in range(HALVES):
                act.wait_ge(att_exp_in, H + 1)
                act.activation(att[:, H, :, :], att[:, H, :, :], ACT.Exp).then_inc(att_exp, 1)
            for H in range(HALVES):
                square(1, H)
            for H in range(HALVES):
                root(1, H)

            act.wait_ge(third_loaded, 16)
            TILES = HALVES * G

            def hidden(i):
                act.wait_ge(fc1_done, i + 1)
                act.activation(tap_view(HALVES + i, CENTRE), rows(ps[:, 0:NB, :].rearrange("p n c -> p (n c)")),
                               ACT.Gelu, bias=c3("fc1_b")).then_inc(hid_gelu, 1)

            def conv_act(i):
                act.wait_ge(conv_done, i + 1)
                act.activation(acc[:, i, :], acc[:, i, :], ACT.Gelu, bias=c3("pos_b")).then_inc(conv_gelu, 1)

            hidden(0)
            hidden(1)
            for pair in range(TILES // 2):
                if 2 * pair + 2 < TILES:
                    hidden(2 * pair + 2)
                    hidden(2 * pair + 3)
                conv_act(2 * pair)
                conv_act(2 * pair + 1)

            def queries(H):
                act.wait_ge(q_proj, H + 1)
                act.activation(m[:, H, :], ps[:, 0:NB, :].rearrange("p n c -> p (n c)"), ACT.Identity,
                               bias=c3("bq")).then_inc(q_ready, 1)

            for H in range(HALVES):
                queries(H)
                for b in range(BH):
                    beta = H * BH + b
                    for gp in range(2):
                        n = 2 * beta + gp
                        act.wait_ge(max_ready, n + 1)
                        if gp == 0 and beta >= 2:
                            act.wait_ge(av_done, beta - 1)
                        for j in range(2):
                            for jt in range(2):
                                g = 2 * gp + j
                                last = act.activation(prob[:, beta % 2, g, jt, :],
                                                      ps[:, 2 + 2 * (n % 2) + j, jt * NPIX:(jt + 1) * NPIX],
                                                      ACT.Exp, scale=-1.0, bias=smin[:, n, 2 * j + jt:2 * j + jt + 1],
                                                      accum_out=psum_row[:, beta, jt, g:g + 1])
                        last.then_inc(exp_done, 1)

        @block.vector
        def _(dve):
            count = [0]

            def link(ins):
                count[0] += 1
                ins.then_inc(dve_chain, 1)
                dve.wait_ge(dve_chain, count[0])

            last_rows = (PROWS - 1 - BH) * ROW
            dve.memset(eps_col[:, :], LN_EPS).then_inc(dve_zeroed, 1)
            dve.memset(padded[:, :, 0:BH * ROW], 0.0).then_inc(dve_zeroed, 1)
            dve.memset(padded[:, :, last_rows:PADDED], 0.0).then_inc(dve_zeroed, 1)
            dve.memset(padded[:, :, BH * ROW:last_rows].rearrange("p n (r s) -> p n r s", s=ROW)[:, :, :, 0:1], 0.0
                       ).then_inc(dve_zeroed, 1)

            def invert(ln, H):
                dve.wait_ge(std_ready, HALVES * ln + H + 1)
                link(dve.reciprocal(rstd_tok[:, ln, H, :], var_tok[:, ln, H, :]))
                dve.tensor_copy(rstd_wide[:, H, :].rearrange("p (t c) -> p t c", c=C),
                                rstd_tok[:, ln, H, :].unsqueeze(2).to_broadcast([P, TOK * G, C])
                                ).then_inc(rstd_ready, 1)

            for H in range(HALVES):
                invert(0, H)
            for H in range(HALVES):
                dve.wait_ge(rstd_spread, H + 1)
                dve.scalar_tensor_tensor(out=tap_view(H, CENTRE), in0=rows(x[:, H, :]), scalar=c1("ln1_w"),
                                         in1=rows(big(H).rearrange("p n c -> p (n c)")), op0=ALU.mult,
                                         op1=ALU.mult).then_inc(normed, 1)
            dve.wait_ge(second_loaded, 16)
            dve.wait_ge(pool_zeroed, 1)

            def attn_taps(H):
                dve.wait_ge(attn_conv_pe, H + 1)
                dve.wait_ge(normed, H + 1)
                dve.wait_ge(dve_zeroed, 4)
                for j, tap in enumerate(ATTN_DVE_TAPS):
                    so_far = big(H).rearrange("p n c -> p (n c)") if j == 0 else acc[:, H, :]
                    ins = dve.scalar_tensor_tensor(out=rows(acc[:, H, :]), in0=tap_view(H, tap),
                                                   scalar=c2("attn_w")[:, tap:tap + 1], in1=rows(so_far),
                                                   op0=ALU.mult, op1=ALU.add)
                    if j < len(ATTN_DVE_TAPS) - 1:
                        link(ins)
                ins.then_inc(attn_conv, 1)

            def pool_keys(H):
                dve.wait_ge(qk_gelu, H + 1)
                k_cols = qk_tok[:, H, :].rearrange("p (a k w g d) -> p a w g d k", a=PAIRS, k=CLASSES, w=2, g=G)
                for pair in range(PAIRS):
                    ins = dve.tensor_reduce(
                        kf[:, H, pair, :].rearrange("p (g s) -> p g s", g=G)[:, :, C - C4:C],
                        k_cols[:, pair, 1, :, :, :], AX_X, ALU.max)
                ins.then_inc(k_pooled, 1)

            def softmax_in(H):
                dve.wait_ge(att_scores, H + 1)
                blocks = ps[:, 4 * H + NB:4 * H + NB + 2, 128:128 + PAIRS * G * C4].rearrange(
                    "p h (a g d) -> p h a g d", a=PAIRS, g=G)
                for g in range(G):
                    ins = dve.tensor_copy(
                        att[C * g:C * (g + 1), H, :, :].rearrange("p (h a) d -> p h a d", h=2),
                        blocks[C * g:C * (g + 1), :, :, g, :])
                link(ins)
                link(dve.tensor_reduce(att_max[:, H, :], att[:, H, :, :], AX_X, ALU.max))
                dve.tensor_tensor(att[:, H, :, :], att[:, H, :, :],
                                  att_max[:, H, :].unsqueeze(2).to_broadcast([P, BH, C4]), ALU.subtract
                                  ).then_inc(att_exp_in, 1)

            def softmax_out(H):
                dve.wait_ge(att_exp, H + 1)
                link(dve.tensor_reduce(att_sum[:, H, :], att[:, H, :, :], AX_X, ALU.add))
                link(dve.reciprocal(att_inv[:, H, :], att_sum[:, H, :]))
                link(dve.tensor_scalar(att_inv[:, H, :], att_inv[:, H, :], c2("is_v"), None, ALU.mult))
                for g in range(G):
                    sl = slice(C * g, C * (g + 1))
                    ins = dve.tensor_tensor(att_blocks[sl, H, :, C * (g + 1) - C4:C * (g + 1)], att[sl, H, :, :],
                                            att_inv[sl, H, :].unsqueeze(2).to_broadcast([C, BH, C4]), ALU.mult)
                ins.then_inc(att_placed, 1)

            for H in range(HALVES):
                pool_keys(H)
            attn_taps(0)
            for H in range(HALVES):
                softmax_in(H)
            attn_taps(1)
            dve.wait_ge(pool_zeroed, 2)
            for H in range(HALVES):
                softmax_out(H)
            for H in range(HALVES):
                dve.wait_ge(att_turned, H + 1)
                dve.tensor_tensor(mix_w[:, H, :, :], small(H, 0).rearrange("p (b c) -> p b c", b=BH),
                                  c2("keep").unsqueeze(1).to_broadcast([P, BH, P]), ALU.add
                                  ).then_inc(mix_ready, 1)
            for H in range(HALVES):
                dve.wait_ge(mixed, H + 1)
                dve.tensor_tensor(by_batch(res1[:, H, :]),
                                  big(H).rearrange("p n (b y s) -> p (n b) y s", y=SIDE, s=SIDE),
                                  by_batch(x[:, H, :]), ALU.add).then_inc(res1_ready, 1)
            for H in range(HALVES):
                invert(1, H)
            for H in range(HALVES):
                dve.wait_ge(rstd_spread, HALVES + H + 1)
                dve.wait_ge(res1_ready, H + 1)
                dve.scalar_tensor_tensor(out=m[:, H, :], in0=res1[:, H, :], scalar=c1("ln2_w"),
                                         in1=big(H).rearrange("p n c -> p (n c)"), op0=ALU.mult,
                                         op1=ALU.mult).then_inc(normed, 1)

            dve.wait_ge(third_loaded, 16)
            TILES = HALVES * G

            def finish_block(H):
                dve.wait_ge(fc2_done, H + 1)
                dve.wait_ge(skip_ready, H + 1)
                dve.tensor_tensor(X[:, H, :], ps[:, 6:8, :].rearrange("p n c -> p (n c)"), skip[:, H, :],
                                  ALU.add).then_inc(X_ready, 1)

            for pair in range(TILES // 2):
                if pair == 3:
                    finish_block(0)
                step = {}
                for j, tap in enumerate(MLP_DVE_TAPS):
                    for i in (2 * pair, 2 * pair + 1):
                        if j == 0:
                            dve.wait_ge(conv_pe, i + 1)
                            so_far = ps[:, 2 + 2 * (i % 2):4 + 2 * (i % 2), :].rearrange("p n c -> p (n c)")
                        else:
                            dve.wait_ge(*step[i])
                            so_far = acc[:, i, :]
                        ins = dve.scalar_tensor_tensor(out=rows(acc[:, i, :]), in0=tap_view(HALVES + i, tap),
                                                       scalar=c3("pos_w")[:, tap:tap + 1], in1=rows(so_far),
                                                       op0=ALU.mult, op1=ALU.add)
                        if j == len(MLP_DVE_TAPS) - 1:
                            ins.then_inc(conv_done, 1)
                        elif j == 0:
                            ins.then_inc(conv_read, 1)
                            step[i] = conv_read, i + 1
                        else:
                            ins.then_inc(dve_chain, 1)
                            count[0] += 1
                            step[i] = dve_chain, count[0]
            finish_block(1)

            def keys_values(H):
                bank = 2 if H == 0 else 0
                dve.wait_ge(k_proj, H + 1)
                for par in range(2):
                    ins = dve.tensor_scalar(k_split[:, par, H, :], ps[:, bank:bank + NB, :].rearrange("p n c -> p (n c)"),
                                            c3("bk"), c3("minus_even" if par == 0 else "minus_odd"),
                                            ALU.add, ALU.mult)
                ins.then_inc(k_ready, 1)
                bank = 4 if H == 0 else 0
                dve.wait_ge(v_proj, H + 1)
                dve.tensor_tensor(v_tok[:, H * BH:(H + 1) * BH, :, :, :].rearrange("p b j g c -> p (b j) (g c)"),
                                  ps[:, bank:bank + NB, :].rearrange("p n (t c) -> p (n t) c", c=P),
                                  c3("bv").unsqueeze(1).to_broadcast([P, 2 * BH, P]), ALU.add).then_inc(v_ready, 1)

            def scale_values(beta):
                dve.wait_ge(exp_done, 2 * beta + 2)
                dve.wait_ge(v_ready, beta // BH + 1)
                link(dve.reciprocal(inv_row[:, beta, :, :], psum_row[:, beta, :, :]))
                v = v_tok[:, beta, :, :, :].rearrange("p j g c -> p (j g) c")
                dve.tensor_tensor(v, v, inv_row[:, beta, :, :].rearrange("p j g -> p (j g)").unsqueeze(2)
                                  .to_broadcast([P, 2 * G, C]), ALU.mult).then_inc(v_scaled, 1)

            def finish(beta):
                H, b = beta // BH, beta % BH
                dve.wait_ge(av_done, beta + 1)
                dve.tensor_tensor(y_out[:, beta, :], ps[:, 6 + beta % 2, 0:NPIX],
                                  X[:, H, b * NPIX:(b + 1) * NPIX], ALU.add).then_inc(y_ready, 1)

            for H in range(HALVES):
                keys_values(H)
                for b in range(BH):
                    beta = H * BH + b
                    for n in (2 * beta, 2 * beta + 1):
                        dve.wait_ge(scores_done, n + 1)
                        bank = 2 + 2 * (n % 2)
                        dve.tensor_reduce(smin[:, n, :], ps[:, bank:bank + 2, :].rearrange(
                            "p n (t i) -> p (n t) i", t=2), AX_X, ALU.min).then_inc(max_ready, 1)
                    if b >= 1:
                        scale_values(beta - 1)
                    if b >= 2:
                        finish(beta - 2)
                scale_values(H * BH + BH - 1)
                finish(H * BH + BH - 2)
                finish(H * BH + BH - 1)


def kernel(x, L0_conv_ln1_w, L0_conv_ln2_w, L0_conv_dw_w, L0_conv_dw_b, L0_conv_qkvl_w, L0_conv_qkvl_b,
           L0_conv_fc1_w, L0_conv_fc1_b, L0_conv_pos_w, L0_conv_pos_b, L0_conv_fc2_w, L0_conv_fc2_b,
           L1_conv_Wq, L1_conv_bq, L1_conv_Wk, L1_conv_bk, L1_conv_Wv, L1_conv_bv):
    import numpy as np
    import concourse.bacc as bacc
    from concourse.bass_utils import run_bass_kernel_spmd

    f = np.float32

    def arr(a):
        return np.asarray(a)

    def tiled(a):
        return np.tile(arr(a).reshape(-1, 1), (G, 1))

    def blocks(w):
        w = arr(w)
        out = np.zeros((P, P), f)
        for g in range(G):
            out[C * g:C * (g + 1), C * g:C * (g + 1)] = w
        return out

    def diagonal(v):
        out = np.zeros((len(v), len(v)), f)
        out[np.arange(len(v)), np.arange(len(v))] = v
        return out

    slot = np.arange(P) % C
    centre = blocks(np.eye(C, dtype=f) - f(1) / f(C))
    ident = np.eye(P, dtype=f)
    mean = np.zeros((P, G), f)
    for g in range(G):
        mean[C * g:C * (g + 1), g] = f(1) / f(C)
    side2 = SIDE // 2
    pool = np.zeros((P, CLASSES, P), f)
    for cl in range(CLASSES):
        for half in range(2):
            for i in range(side2):
                for j in range(side2):
                    for a in ((i,) if cl // 2 == 0 else (i - 1, i)):
                        for b in ((j,) if cl % 2 == 0 else (j - 1, j)):
                            if a >= 0 and b >= 0:
                                pool[half * POOLED + a * side2 + b, cl, half * POOLED + i * side2 + j] = 1
    keep = diagonal((slot < C - C4).astype(f))
    is_v = (slot >= C - C4).astype(f).reshape(P, 1)
    parity = (np.arange(P) // C) % 2
    minus_even = np.where(parity == 0, f(-1), f(0)).astype(f).reshape(P, 1)
    minus_odd = np.where(parity == 1, f(-1), f(0)).astype(f).reshape(P, 1)
    ones = np.zeros((P, P), f)
    ones[0] = 1

    dw = arr(L0_conv_dw_w).reshape(C2, 9)
    wall = arr(L0_conv_qkvl_w).reshape(4, C4, C2)
    ball = arr(L0_conv_qkvl_b).reshape(4, C4)
    taps = []
    for tap in ATTN_PE_TAPS:
        w = np.zeros((C, C), f)
        w[:C2, :C2] = diagonal(dw[:, tap])
        if tap == CENTRE:
            w[C2:, C2:C2 + C4] = wall[3].T
            w[C2:, C2 + C4:] = wall[2].T
        taps.append(blocks(w))
    attn_w = np.zeros((C, 9), f)
    attn_w[:C2] = dw
    attn_b = np.concatenate([arr(L0_conv_dw_b), ball[3], ball[2]])
    qk_w = np.zeros((P, 2, G, C4), f)
    qk_brow = np.zeros((P, 2, G, C4), f)
    for g in range(G):
        for which in range(2):
            qk_w[C * g + C2:C * (g + 1), which, g] = wall[which].T
            qk_brow[0, which, g] = ball[which]

    fc1 = arr(L0_conv_fc1_w).reshape(HID, C).T
    fc1_w = np.zeros((P, 2, HID), f)
    for g in range(G):
        fc1_w[C * g:C * (g + 1), g % 2] = fc1
    pos = arr(L0_conv_pos_w).reshape(HID, 9)

    def side_by_side(cols, n, **parts):
        out = np.zeros((P, n), f)
        for name, (a, b) in cols.items():
            out[:, a:b] = parts[name].reshape(P, b - a)
        return out

    first = side_by_side(FIRST_COLS, FIRST_N, centre=centre, ident=ident, mean=mean,
                         ln1_w=tiled(L0_conv_ln1_w), ln2_w=tiled(L0_conv_ln2_w))
    second = side_by_side(SECOND_COLS, SECOND_N, attn_taps=np.concatenate(taps, 1), attn_w=np.tile(attn_w, (G, 1)),
                          attn_b=tiled(attn_b), qk_w=qk_w, qk_brow=qk_brow, ones=ones, pool=pool, keep=keep,
                          is_v=is_v)
    third = side_by_side(THIRD_COLS, THIRD_N, fc1_w=fc1_w, fc1_b=arr(L0_conv_fc1_b),
                         mlp_taps=np.concatenate([diagonal(pos[:, t]) for t in MLP_PE_TAPS], 1), pos_w=pos,
                         pos_b=arr(L0_conv_pos_b), fc2_w=arr(L0_conv_fc2_w).reshape(C, HID).T,
                         fc2_b=tiled(L0_conv_fc2_b), wq=blocks(arr(L1_conv_Wq).T), wk=blocks(arr(L1_conv_Wk).T),
                         wv=blocks(arr(L1_conv_Wv).T), bq=tiled(L1_conv_bq), bk=tiled(L1_conv_bk),
                         bv=np.broadcast_to(np.tile(arr(L1_conv_bv), G), (P, P)),
                         minus_even=minus_even, minus_odd=minus_odd)
    xs = arr(x).reshape(G, HALVES, BH, C, SIDE, SIDE).transpose(0, 3, 1, 4, 2, 5).reshape(P, HALVES * COLS)

    nc = bacc.Bacc("TRN2", target_bir_lowering=False, num_devices=1)
    arrays = {"x_in": np.ascontiguousarray(xs), "first_in": first, "second_in": second, "third_in": third}
    args = [nc.dram_tensor(n, a.shape, F32, kind="ExternalInput").ap() for n, a in arrays.items()]
    args.append(nc.dram_tensor("y", (P, HALVES * COLS), F32, kind="ExternalOutput").ap())
    build(nc, *args)
    r = run_bass_kernel_spmd(nc, [arrays], core_ids=[0])
    y = np.asarray(r.results[0]["y"]).reshape(G, C, HALVES, BH, SIDE, SIDE)
    return y.transpose(0, 2, 3, 1, 4, 5).reshape(B, C, SIDE, SIDE)
```

```python
from contextlib import ExitStack

import concourse.bass as bass
from concourse import mybir

ALU = mybir.AluOpType
ACT = mybir.ActivationFunctionType
F32 = mybir.dt.float32
AX_X = mybir.AxisListType.X

P = 128
C = 32
G = P // C
B = 32
SIDE = 16
NPIX = SIDE * SIDE
HALVES = 2
BH = B // G // HALVES
COLS = BH * NPIX
BANK = 512
NB = COLS // BANK
C2, C4 = C // 2, C // 4
HID = 128
ROW = SIDE + 1
PROWS = (SIDE + 2) * BH + 1
PADDED = PROWS * ROW
INNER = BH * ROW + 1
ROWS = SIDE * BH
PAIRS = BH // 2
CLASSES = 4
POOLED = NPIX // 4
GROUPS = HALVES * BH * 2
DEEP = 3
BATCH_ORDER = [0, 2, 1, 3]
LN_EPS = 1e-5

TAPS = [(dy, dx) for dy in (-1, 0, 1) for dx in (-1, 0, 1)]
CENTRE = 4
ATTN_PE_TAPS = [4, 0, 1, 2]
ATTN_DVE_TAPS = [t for t in range(9) if t not in ATTN_PE_TAPS]
MLP_PE_TAPS = [2, 2, 3, 3, 3, 4, 4, 5]


def columns(sizes):
    at, out = 0, {}
    for name, n in sizes:
        out[name] = (at, at + n)
        at += n
    return out, at


FIRST_COLS, FIRST_N = columns([("centre", P), ("ident", P), ("mean", P), ("ln1_w", 1), ("ln2_w", 1)])
SECOND_COLS, SECOND_N = columns([
    ("attn_taps", P * len(ATTN_PE_TAPS)), ("attn_w", 9), ("attn_b", 1), ("qk_w", 2 * G * C4),
    ("qk_brow", 2 * G * C4), ("ones", P), ("pool", CLASSES * P), ("keep", P), ("is_v", 1),
])
THIRD_COLS, THIRD_N = columns([
    ("fc1_w", G * HID), ("fc1_b", 1), ("mlp_taps", P * 9), ("pos_w", 9), ("pos_b", 1),
    ("fc2_w", C), ("fc2_b", 1), ("wq", P), ("wk", P), ("wv", P), ("bq", 1), ("bk", 1), ("bv", P),
    ("minus_own", G),
])


def build(nc, x_in, first_in, second_in, third_in, out):
    with ExitStack() as ctx:
        def sb(name, shape):
            return ctx.enter_context(nc.sbuf_tensor(name, shape, F32))

        def sem(name):
            return ctx.enter_context(nc.semaphore(name))

        ps = ctx.enter_context(nc.psum_tensor("ps", [P, 8, BANK], F32))

        x = sb("x", [P, HALVES, COLS])
        first = sb("first", [P, FIRST_N])
        second = sb("second", [P, SECOND_N])
        third = sb("third", [P, THIRD_N])
        padded = sb("padded", [P, HALVES * (1 + G), PADDED])
        acc = sb("acc", [P, HALVES * G, COLS])
        norm_parity = acc[:, 4:6, :].rearrange("p h (k n) -> p h k n", k=CLASSES)
        rstd = acc[:, 6:8, :]
        eps_col = sb("eps_col", [P, 1])
        qk_tok = sb("qk_tok", [P, HALVES, PAIRS * CLASSES * 2 * G * C4])
        kf = sb("kf", [P, HALVES, PAIRS, P])
        qf = sb("qf", [P, HALVES, PAIRS, G * C4])
        att = sb("att", [P, HALVES, BH, C4])
        att_max = sb("att_max", [P, HALVES, BH])
        att_sum = sb("att_sum", [P, HALVES, BH])
        att_inv = sb("att_inv", [P, HALVES, BH])
        att_blocks = sb("att_blocks", [P, HALVES, BH, P])
        mix_w = sb("mix_w", [P, HALVES, BH, P])
        res1 = sb("res1", [P, HALVES, COLS])
        skip = sb("skip", [P, HALVES, COLS])
        m = sb("m", [P, HALVES, COLS])
        X = sb("X", [P, HALVES, COLS])
        k_split = padded[:, :, :].rearrange("p n c -> p (n c)")[:, 0:G * HALVES * COLS].rearrange(
            "p (g h c) -> p g h c", g=G, h=HALVES)
        v_tok = sb("v_tok", [P, HALVES * BH, 2, G, C])
        prob = sb("prob", [P, 2, G, 2, NPIX])
        k_bias = sb("k_bias", [P, G])
        smin = sb("smin", [P, HALVES * BH * 2, 4])
        psum_row = sb("psum_row", [P, HALVES * BH, 2, G])
        inv_row = sb("inv_row", [P, HALVES * BH, 2, G])
        y_out = sb("y_out", [P, HALVES * BH, NPIX])

        def c1(name):
            return first[:, FIRST_COLS[name][0]:FIRST_COLS[name][1]]

        def c2(name):
            return second[:, SECOND_COLS[name][0]:SECOND_COLS[name][1]]

        def c3(name):
            return third[:, THIRD_COLS[name][0]:THIRD_COLS[name][1]]

        def big(H, n=NB):
            return ps[:, 4 * H:4 * H + n, :]

        def small(H, which):
            return ps[:, 4 * H + NB + which, :]

        def tap_view(buf, tap, bank=None):
            dy, dx = TAPS[tap]
            off = INNER + dy * BH * ROW + dx
            n = ROWS if bank is None else ROWS // NB
            off += 0 if bank is None else bank * n * ROW
            return padded[:, buf, off:off + n * ROW].rearrange("p (r s) -> p r s", s=ROW)[:, :, 0:SIDE]

        def rows(ap):
            return ap.rearrange("p (r s) -> p r s", s=SIDE)

        def by_batch(ap):
            return ap.rearrange("p (y b s) -> p b y s", b=BH, s=SIDE)

        x_loaded = [sem(f"x_loaded{H}") for H in range(HALVES)]
        first_loaded, second_loaded, third_loaded = sem("first_loaded"), sem("second_loaded"), sem("third_loaded")
        dve_zeroed, pool_zeroed = sem("dve_zeroed"), sem("pool_zeroed")
        parity_split, skip_ready = sem("parity_split"), sem("skip_ready")
        centred, squared, var_ready = sem("centred"), sem("squared"), sem("var_ready")
        log_ready, rstd_ready, normed = sem("log_ready"), sem("rstd_ready"), sem("normed")
        attn_conv_pe, qk_proj, qk_gelu, k_pooled = (
            sem("attn_conv_pe"), sem("qk_proj"), sem("qk_gelu"), sem("k_pooled"))
        q_pooled, q_scaled, att_scores, att_exp_in, att_exp = (
            sem("q_pooled"), sem("q_scaled"), sem("att_scores"), sem("att_exp_in"), sem("att_exp"))
        att_placed, att_turned, mix_ready, attn_sum, attn_gelu, mixed, res1_ready = (
            sem("att_placed"), sem("att_turned"), sem("mix_ready"), sem("attn_sum"), sem("attn_gelu"),
            sem("mixed"), sem("res1_ready"))
        fc1_done, hid_gelu, conv_pe, conv_read, conv_done, conv_gelu, fc2_done, X_ready = (
            sem("fc1_done"), sem("hid_gelu"), sem("conv_pe"), sem("conv_read"), sem("conv_done"),
            sem("conv_gelu"), sem("fc2_done"), sem("X_ready"))
        q_proj, q_ready, k_proj, k_low_ready, k_ready, v_proj, v_ready = (
            sem("q_proj"), sem("q_ready"), sem("k_proj"), sem("k_low_ready"), sem("k_ready"), sem("v_proj"), sem("v_ready"))
        scores_done, max_ready, exp_done, v_scaled, av_done, y_ready, stored = (
            sem("scores_done"), sem("max_ready"), sem("exp_done"), sem("v_scaled"), sem("av_done"),
            sem("y_ready"), sem("stored"))
        dve_chain = sem("dve_chain")

        block = ctx.enter_context(nc.Block())

        @block.sync
        def _(sp):
            for H in range(HALVES):
                sp.dma_start(x[:, H, :], x_in[:, H * COLS:(H + 1) * COLS]).then_inc(x_loaded[H], 16)
            sp.dma_start(second[:, :], second_in).then_inc(second_loaded, 16)
            sp.dma_start(third[:, :], third_in).then_inc(third_loaded, 16)
            for beta in range(HALVES * BH):
                sp.wait_ge(y_ready, beta + 1)
                sp.dma_start(out[:, beta * NPIX:(beta + 1) * NPIX], y_out[:, beta, :]).then_inc(stored, 16)
            sp.wait_ge(stored, 16 * HALVES * BH)

        @block.gpsimd
        def _(pool):
            pool.memset(kf[:, :, :, :], 0.0).then_inc(pool_zeroed, 1)
            pool.memset(att_blocks[:, :, :, :], 0.0).then_inc(pool_zeroed, 1)
            pool.wait_ge(third_loaded, 16)
            for H in range(HALVES):
                pool.wait_ge(res1_ready, H + 1)
                pool.tensor_scalar(skip[:, H, :].rearrange("p (b y s) -> p b y s", b=BH, s=SIDE),
                                   by_batch(res1[:, H, :]), c3("fc2_b"), None, ALU.add).then_inc(skip_ready, 1)

        @block.tensor
        def _(pe):
            def centre(ln, H, src):
                for n in range(NB):
                    last = pe.matmul(big(H)[:, n, :], c1("centre"), src[:, H, n * BANK:(n + 1) * BANK],
                                     start=True, stop=True)
                last.then_inc(centred, 1)

            def variance(ln, H):
                pe.wait_ge(squared, HALVES * ln + H + 1)
                for n in range(NB):
                    last = pe.matmul(big(H)[:, n, :], c1("mean"), acc[:, 2 + H, n * BANK:(n + 1) * BANK],
                                     start=True, stop=True)
                last.then_inc(var_ready, 1)

            pe.wait_ge(first_loaded, 16)
            for H in range(HALVES):
                pe.wait_ge(x_loaded[H], 16)
                centre(0, H, x)
            for H in range(HALVES):
                variance(0, H)

            pe.wait_ge(second_loaded, 16)
            pe.wait_ge(dve_zeroed, 4)
            for H in range(HALVES):
                pe.wait_ge(parity_split, H + 1)
                pe.matmul(small(H, 0), c2("ones")[0:1, :],
                          c2("qk_brow")[0:1, :].unsqueeze(1).to_broadcast([1, PAIRS * CLASSES, 2 * G * C4]),
                          start=True, stop=False)
                for pair in range(PAIRS):
                    for cl in range(CLASSES):
                        at = (pair * CLASSES + cl) * 2 * G * C4
                        last = pe.matmul(small(H, 0)[:, at:at + 2 * G * C4],
                                         norm_parity[:, H, cl, pair * P:(pair + 1) * P],
                                         c2("qk_w"), start=False, stop=(pair, cl) == (PAIRS - 1, CLASSES - 1))
                last.then_inc(qk_proj, 1)
                pe.wait_ge(normed, H + 1)
                for n in range(NB):
                    for i, tap in enumerate(ATTN_PE_TAPS):
                        last = pe.matmul(big(H)[:, n, :], c2("attn_taps")[:, i * P:(i + 1) * P],
                                         tap_view(H, tap, n), start=i == 0, stop=i == len(ATTN_PE_TAPS) - 1)
                last.then_inc(attn_conv_pe, 1)
            pe.wait_ge(pool_zeroed, 2)
            for H in range(HALVES):
                pe.wait_ge(qk_gelu, H + 1)
                q_cols = qk_tok[:, H, :].rearrange("p (a k w d) -> p a k w d", a=PAIRS, k=CLASSES, w=2)
                for cl in range(CLASSES):
                    last = pe.matmul(small(H, 1)[:, 64:64 + PAIRS * G * C4], c2("pool")[:, cl * P:(cl + 1) * P],
                                     q_cols[:, :, cl, 0, :], start=cl == 0, stop=cl == CLASSES - 1)
                last.then_inc(q_pooled, 1)
            for H in range(HALVES):
                pe.wait_ge(k_pooled, H + 1)
                pe.wait_ge(q_scaled, H + 1)
                for b in BATCH_ORDER:
                    pair, half = b // 2, b % 2
                    lo = POOLED * half
                    last = pe.matmul(small(H, half)[:, 128 + pair * G * C4:128 + (pair + 1) * G * C4],
                                     kf[lo:lo + POOLED, H, pair, :], qf[lo:lo + POOLED, H, pair, :],
                                     start=True, stop=True)
                last.then_inc(att_scores, 1)
            for H in range(HALVES):
                pe.wait_ge(att_placed, H + 1)
                for b in range(BH):
                    last = pe.transpose(small(H, 0)[:, b * P:(b + 1) * P], att_blocks[:, H, b, :], c1("ident"))
                last.then_inc(att_turned, 1)
            for H in range(HALVES):
                pe.wait_ge(mix_ready, H + 1)
                pe.wait_ge(attn_gelu, H + 1)
                for s, b in enumerate(BATCH_ORDER):
                    at = b * NPIX
                    last = pe.matmul(big(H)[:, at // BANK, at % BANK:at % BANK + NPIX], mix_w[:, H, s, :],
                                     by_batch(acc[:, H, :])[:, b, :, :], start=True, stop=True)
                last.then_inc(mixed, 1)
            for H in range(HALVES):
                pe.wait_ge(res1_ready, H + 1)
                centre(1, H, res1)
            for H in range(HALVES):
                variance(1, H)

            pe.wait_ge(third_loaded, 16)
            TILES = HALVES * G

            def fc1(i):
                H, g = i // G, i % G
                pe.wait_ge(normed, HALVES + H + 1)
                if i >= 1:
                    pe.wait_ge(hid_gelu, i)
                w = c3("fc1_w")[:, g * HID:(g + 1) * HID]
                for n in range(NB):
                    last = pe.matmul(ps[:, n, :], w, m[:, H, n * BANK:(n + 1) * BANK],
                                     start=True, stop=True)
                last.then_inc(fc1_done, 1)

            def conv(i):
                pe.wait_ge(hid_gelu, i + 1)
                if i == 0:
                    pe.wait_ge(normed, 2 * HALVES)
                if i >= 2:
                    pe.wait_ge(conv_read, i - 1)
                for n in range(NB):
                    for tap in range(MLP_PE_TAPS[i]):
                        last = pe.matmul(ps[:, 2 + 2 * (i % 2) + n, :], c3("mlp_taps")[:, tap * P:(tap + 1) * P],
                                         tap_view(HALVES + i, tap, n), start=tap == 0,
                                         stop=tap == MLP_PE_TAPS[i] - 1)
                last.then_inc(conv_pe, 1)

            def fc2(H):
                pe.wait_ge(conv_gelu, G * (H + 1))
                if H:
                    pe.wait_ge(X_ready, H)
                for n in range(NB):
                    for part in range(2):
                        for g in range(G):
                            i = G * H + g
                            h = padded[:, HALVES + i, INNER:INNER + ROWS * ROW].rearrange(
                                "p (y b s) -> p b y s", b=BH, s=ROW)[:, :, :, 0:SIDE]
                            rhs = (h, by_batch(acc[:, i, :]))[part][:, 2 * n:2 * n + 2, :, :]
                            last = pe.matmul(ps[C * g:C * (g + 1), 6 + n, :], c3("fc2_w"), rhs,
                                             start=part == 0, stop=part == 1)
                last.then_inc(fc2_done, 1)

            fc1(0)
            fc1(1)
            for pair in range(TILES // 2):
                if pair == 3:
                    fc2(0)
                conv(2 * pair)
                conv(2 * pair + 1)
                if 2 * pair + 2 < TILES:
                    fc1(2 * pair + 2)
                    fc1(2 * pair + 3)
            fc2(1)

            def channel_proj(name, done, H, bank):
                for n in range(NB):
                    last = pe.matmul(ps[:, bank + n, :], c3(name), X[:, H, n * BANK:(n + 1) * BANK],
                                     start=True, stop=True)
                last.then_inc(done, 1)

            def value_proj(H, bank):
                for b in range(BH):
                    for jt in range(2):
                        at = (2 * b + jt) * P
                        last = pe.matmul(ps[:, bank + at // BANK, at % BANK:at % BANK + P],
                                         X[:, H, at:at + P], c3("wv"),
                                         start=True, stop=True)
                last.then_inc(v_proj, 1)

            def scores(n):
                H, b, gp = n // (2 * BH), n // 2 % BH, n % 2
                if n >= DEEP:
                    pe.wait_ge(exp_done, n - DEEP + 1)
                for j in range(2):
                    for jt in range(2):
                        at = b * NPIX + jt * P
                        k = k_split[:, 2 * gp + j, H, at:at + P]
                        q = m[:, H, b * NPIX:(b + 1) * NPIX]
                        last = pe.matmul(ps[:, 2 * (n % DEEP) + j, jt * NPIX:(jt + 1) * NPIX], k, q,
                                         start=True, stop=True)
                last.then_inc(scores_done, 1)

            def weighted_values(beta):
                pe.wait_ge(v_scaled, beta + 1)
                if beta >= 2:
                    pe.wait_ge(y_ready, beta - 1)
                for jt in range(2):
                    for g in range(G):
                        last = pe.matmul(ps[C * g:C * (g + 1), 6 + beta % 2, 0:NPIX], v_tok[:, beta, jt, g, :],
                                         prob[:, beta % 2, g, jt, :], start=jt == 0, stop=jt == 1)
                last.then_inc(av_done, 1)

            pe.wait_ge(X_ready, HALVES)
            channel_proj("wq", q_proj, 0, 0)
            channel_proj("wk", k_proj, 0, 2)
            channel_proj("wq", q_proj, 1, 6)
            pe.wait_ge(q_ready, 1)
            channel_proj("wk", k_proj, 1, 0)
            value_proj(0, 4)
            pe.wait_ge(k_ready, 1)
            value_proj(1, 2)
            pe.wait_ge(q_ready, 2)
            pe.wait_ge(k_ready, 2)
            pe.wait_ge(v_ready, 2)
            for n in range(DEEP):
                scores(n)
            for beta in range(HALVES * BH):
                if 2 * beta + DEEP < GROUPS:
                    scores(2 * beta + DEEP)
                if beta >= 1:
                    weighted_values(beta - 1)
                if 2 * beta + DEEP + 1 < GROUPS:
                    scores(2 * beta + DEEP + 1)
            weighted_values(HALVES * BH - 1)

        @block.scalar
        def _(act):
            def square(ln, H):
                act.wait_ge(centred, HALVES * ln + H + 1)
                act.activation(acc[:, 2 + H, :], big(H).rearrange("p n c -> p (n c)"),
                               ACT.Square).then_inc(squared, 1)

            def inverse_root(ln, H):
                act.wait_ge(var_ready, HALVES * ln + H + 1)
                act.activation(rstd[:, H, :], big(H).rearrange("p n c -> p (n c)"), ACT.Ln,
                               bias=eps_col[:, :]).then_inc(log_ready, 1)
                act.wait_ge(log_ready, HALVES * ln + H + 1)
                act.activation(rstd[:, H, :], rstd[:, H, :], ACT.Exp, scale=-0.5).then_inc(rstd_ready, 1)

            act.dma_start(first[:, :], first_in).then_inc(first_loaded, 16)
            act.preload_act_table_set("natural_log_exp_and_others")
            act.wait_ge(dve_zeroed, 4)
            for H in range(HALVES):
                square(0, H)
            for H in range(HALVES):
                inverse_root(0, H)
            for H in range(HALVES):
                act.wait_ge(normed, H + 1)
                whole = padded[:, H, INNER:INNER + ROWS * ROW].rearrange("p (y b s) -> p b y s", b=BH, s=ROW)
                for cl in range(CLASSES):
                    last = act.activation(
                        norm_parity[:, H, cl, :].rearrange("p (b i j) -> p b i j", b=BH, j=SIDE // 2),
                        whole[:, :, cl // 2::2, cl % 2:SIDE:2], ACT.Copy)
                last.then_inc(parity_split, 1)
            act.wait_ge(second_loaded, 16)
            for H in range(HALVES):
                act.wait_ge(qk_proj, H + 1)
                act.activation(qk_tok[:, H, :], small(H, 0), ACT.Gelu).then_inc(qk_gelu, 1)
            for H in range(HALVES):
                act.wait_ge(q_pooled, H + 1)
                act.activation(qf[:, H, :, :].rearrange("p a d -> p (a d)"),
                               small(H, 1)[:, 64:64 + PAIRS * G * C4], ACT.Copy, scale=1.0 / 9.0
                               ).then_inc(q_scaled, 1)
            for H in range(HALVES):
                act.wait_ge(att_exp_in, H + 1)
                act.activation(att[:, H, :, :], att[:, H, :, :], ACT.Exp).then_inc(att_exp, 1)
            for H in range(HALVES):
                act.wait_ge(attn_sum, len(ATTN_DVE_TAPS) * (H + 1))
                act.activation(acc[:, H, :], acc[:, H, :], ACT.Gelu, bias=c2("attn_b")).then_inc(attn_gelu, 1)
            act.preload_act_table_set("natural_log_exp_and_others")
            for H in range(HALVES):
                square(1, H)
            for H in range(HALVES):
                inverse_root(1, H)

            act.wait_ge(third_loaded, 16)
            TILES = HALVES * G

            def hidden(i):
                act.wait_ge(fc1_done, i + 1)
                act.activation(tap_view(HALVES + i, CENTRE), rows(ps[:, 0:NB, :].rearrange("p n c -> p (n c)")),
                               ACT.Gelu, bias=c3("fc1_b")).then_inc(hid_gelu, 1)

            def conv_act(i):
                act.wait_ge(conv_done, i + 1)
                act.activation(acc[:, i, :], acc[:, i, :], ACT.Gelu, bias=c3("pos_b")).then_inc(conv_gelu, 1)

            hidden(0)
            hidden(1)
            for pair in range(TILES // 2):
                if 2 * pair + 2 < TILES:
                    hidden(2 * pair + 2)
                    hidden(2 * pair + 3)
                conv_act(2 * pair)
                conv_act(2 * pair + 1)

            def queries(H):
                act.wait_ge(q_proj, H + 1)
                act.activation(m[:, H, :], ps[:, 6 * H:6 * H + NB, :].rearrange("p n c -> p (n c)"), ACT.Identity,
                               bias=c3("bq")).then_inc(q_ready, 1)

            def high_keys(H):
                bank = 2 if H == 0 else 0
                act.wait_ge(k_low_ready, H + 1)
                for g in range(2, G):
                    last = act.activation(k_split[:, g, H, :], ps[:, bank:bank + NB, :].rearrange("p n c -> p (n c)"),
                                          ACT.Identity, scale=c3("minus_own")[:, g:g + 1], bias=k_bias[:, g:g + 1])
                last.then_inc(k_ready, 1)

            queries(0)
            queries(1)
            high_keys(0)
            high_keys(1)
            for H in range(HALVES):
                for b in range(BH):
                    beta = H * BH + b
                    for gp in range(2):
                        n = 2 * beta + gp
                        act.wait_ge(max_ready, n + 1)
                        if gp == 0 and beta >= 2:
                            act.wait_ge(av_done, beta - 1)
                        for j in range(2):
                            for jt in range(2):
                                g = 2 * gp + j
                                last = act.activation(prob[:, beta % 2, g, jt, :],
                                                      ps[:, 2 * (n % DEEP) + j, jt * NPIX:(jt + 1) * NPIX],
                                                      ACT.Exp, scale=-1.0, bias=smin[:, n, 2 * j + jt:2 * j + jt + 1],
                                                      accum_out=psum_row[:, beta, jt, g:g + 1])
                        last.then_inc(exp_done, 1)

        @block.vector
        def _(dve):
            count = [0]

            def link(ins):
                count[0] += 1
                ins.then_inc(dve_chain, 1)
                dve.wait_ge(dve_chain, count[0])

            last_rows = (PROWS - 1 - BH) * ROW
            dve.memset(eps_col[:, :], LN_EPS).then_inc(dve_zeroed, 1)
            dve.memset(padded[:, :, 0:BH * ROW], 0.0).then_inc(dve_zeroed, 1)
            dve.memset(padded[:, :, last_rows:PADDED], 0.0).then_inc(dve_zeroed, 1)
            dve.memset(padded[:, :, BH * ROW:last_rows].rearrange("p n (r s) -> p n r s", s=ROW)[:, :, :, 0:1], 0.0
                       ).then_inc(dve_zeroed, 1)

            for H in range(HALVES):
                dve.wait_ge(rstd_ready, H + 1)
                dve.scalar_tensor_tensor(out=tap_view(H, CENTRE), in0=rows(x[:, H, :]), scalar=c1("ln1_w"),
                                         in1=rows(rstd[:, H, :]), op0=ALU.mult, op1=ALU.mult
                                         ).then_inc(normed, 1)
            dve.wait_ge(second_loaded, 16)
            dve.wait_ge(pool_zeroed, 1)

            def attn_tap(H, j):
                if j == 0:
                    dve.wait_ge(attn_conv_pe, H + 1)
                    dve.wait_ge(normed, H + 1)
                    dve.wait_ge(dve_zeroed, 4)
                    so_far = big(H).rearrange("p n c -> p (n c)")
                else:
                    dve.wait_ge(attn_sum, len(ATTN_DVE_TAPS) * H + j)
                    so_far = acc[:, H, :]
                tap = ATTN_DVE_TAPS[j]
                dve.scalar_tensor_tensor(out=rows(acc[:, H, :]), in0=tap_view(H, tap),
                                         scalar=c2("attn_w")[:, tap:tap + 1], in1=rows(so_far),
                                         op0=ALU.mult, op1=ALU.add).then_inc(attn_sum, 1)

            def pool_keys(H):
                dve.wait_ge(qk_gelu, H + 1)
                k_cols = qk_tok[:, H, :].rearrange("p (a k w g d) -> p a w g d k", a=PAIRS, k=CLASSES, w=2, g=G)
                for pair in range(PAIRS):
                    ins = dve.tensor_reduce(
                        kf[:, H, pair, :].rearrange("p (g s) -> p g s", g=G)[:, :, C - C4:C],
                        k_cols[:, pair, 1, :, :, :], AX_X, ALU.max)
                ins.then_inc(k_pooled, 1)

            def softmax_in(H):
                dve.wait_ge(att_scores, H + 1)
                blocks = ps[:, 4 * H + NB:4 * H + NB + 2, 128:128 + PAIRS * G * C4].rearrange(
                    "p h (a g d) -> p h a g d", a=PAIRS, g=G)
                for g in range(G):
                    ins = dve.tensor_copy(
                        att[C * g:C * (g + 1), H, :, :].rearrange("p (h a) d -> p h a d", h=2),
                        blocks[C * g:C * (g + 1), :, :, g, :])
                link(ins)
                link(dve.tensor_reduce(att_max[:, H, :], att[:, H, :, :], AX_X, ALU.max))
                dve.tensor_tensor(att[:, H, :, :], att[:, H, :, :],
                                  att_max[:, H, :].unsqueeze(2).to_broadcast([P, BH, C4]), ALU.subtract
                                  ).then_inc(att_exp_in, 1)

            def softmax_out(H):
                dve.wait_ge(att_exp, H + 1)
                link(dve.tensor_reduce(att_sum[:, H, :], att[:, H, :, :], AX_X, ALU.add))
                link(dve.reciprocal(att_inv[:, H, :], att_sum[:, H, :]))
                link(dve.tensor_scalar(att_inv[:, H, :], att_inv[:, H, :], c2("is_v"), None, ALU.mult))
                for g in range(G):
                    sl = slice(C * g, C * (g + 1))
                    ins = dve.tensor_tensor(att_blocks[sl, H, :, C * (g + 1) - C4:C * (g + 1)], att[sl, H, :, :],
                                            att_inv[sl, H, :].unsqueeze(2).to_broadcast([C, BH, C4]), ALU.mult)
                ins.then_inc(att_placed, 1)

            n_taps = len(ATTN_DVE_TAPS)
            pool_keys(0)
            pool_keys(1)
            attn_tap(0, 0)
            attn_tap(0, 1)
            softmax_in(0)
            for j in range(2, n_taps):
                attn_tap(0, j)
            softmax_in(1)
            attn_tap(1, 0)
            dve.wait_ge(pool_zeroed, 2)
            softmax_out(0)
            attn_tap(1, 1)
            softmax_out(1)
            for j in range(2, n_taps):
                attn_tap(1, j)
            for H in range(HALVES):
                dve.wait_ge(att_turned, H + 1)
                dve.tensor_tensor(mix_w[:, H, :, :], small(H, 0).rearrange("p (b c) -> p b c", b=BH),
                                  c2("keep").unsqueeze(1).to_broadcast([P, BH, P]), ALU.add
                                  ).then_inc(mix_ready, 1)
            for H in range(HALVES):
                dve.wait_ge(mixed, H + 1)
                dve.tensor_tensor(by_batch(res1[:, H, :]),
                                  big(H).rearrange("p n (b y s) -> p (n b) y s", y=SIDE, s=SIDE),
                                  by_batch(x[:, H, :]), ALU.add).then_inc(res1_ready, 1)
            for H in range(HALVES):
                dve.wait_ge(rstd_ready, HALVES + H + 1)
                dve.wait_ge(res1_ready, H + 1)
                dve.scalar_tensor_tensor(out=m[:, H, :], in0=res1[:, H, :], scalar=c1("ln2_w"),
                                         in1=rstd[:, H, :], op0=ALU.mult, op1=ALU.mult
                                         ).then_inc(normed, 1)

            dve.wait_ge(third_loaded, 16)
            dve.tensor_scalar(k_bias[:, :], c3("minus_own"), c3("bk"), None, ALU.mult)
            TILES = HALVES * G

            def finish_block(H):
                dve.wait_ge(fc2_done, H + 1)
                dve.wait_ge(skip_ready, H + 1)
                dve.tensor_tensor(X[:, H, :], ps[:, 6:8, :].rearrange("p n c -> p (n c)"), skip[:, H, :],
                                  ALU.add).then_inc(X_ready, 1)

            for pair in range(TILES // 2):
                if pair == 3:
                    finish_block(0)
                step = {}
                for tap in range(9):
                    for i in (2 * pair, 2 * pair + 1):
                        if tap < MLP_PE_TAPS[i]:
                            continue
                        if tap == MLP_PE_TAPS[i]:
                            dve.wait_ge(conv_pe, i + 1)
                            so_far = ps[:, 2 + 2 * (i % 2):4 + 2 * (i % 2), :].rearrange("p n c -> p (n c)")
                        else:
                            dve.wait_ge(*step[i])
                            so_far = acc[:, i, :]
                        ins = dve.scalar_tensor_tensor(out=rows(acc[:, i, :]), in0=tap_view(HALVES + i, tap),
                                                       scalar=c3("pos_w")[:, tap:tap + 1], in1=rows(so_far),
                                                       op0=ALU.mult, op1=ALU.add)
                        if tap == 8:
                            ins.then_inc(conv_done, 1)
                        elif tap == MLP_PE_TAPS[i]:
                            ins.then_inc(conv_read, 1)
                            step[i] = conv_read, i + 1
                        else:
                            ins.then_inc(dve_chain, 1)
                            count[0] += 1
                            step[i] = dve_chain, count[0]
            finish_block(1)

            def keys(H):
                bank = 2 if H == 0 else 0
                dve.wait_ge(k_proj, H + 1)
                for g in range(2):
                    ins = dve.tensor_scalar(k_split[:, g, H, :], ps[:, bank:bank + NB, :].rearrange("p n c -> p (n c)"),
                                            c3("bk"), c3("minus_own")[:, g:g + 1], ALU.add, ALU.mult)
                ins.then_inc(k_low_ready, 1)

            def values(H):
                bank = 4 if H == 0 else 2
                dve.wait_ge(v_proj, H + 1)
                dve.tensor_tensor(v_tok[:, H * BH:(H + 1) * BH, :, :, :].rearrange("p b j g c -> p (b j) (g c)"),
                                  ps[:, bank:bank + NB, :].rearrange("p n (t c) -> p (n t) c", c=P),
                                  c3("bv").unsqueeze(1).to_broadcast([P, 2 * BH, P]), ALU.add).then_inc(v_ready, 1)

            def scale_values(beta):
                dve.wait_ge(exp_done, 2 * beta + 2)
                dve.wait_ge(v_ready, beta // BH + 1)
                link(dve.reciprocal(inv_row[:, beta, :, :], psum_row[:, beta, :, :]))
                v = v_tok[:, beta, :, :, :].rearrange("p j g c -> p (j g) c")
                dve.tensor_tensor(v, v, inv_row[:, beta, :, :].rearrange("p j g -> p (j g)").unsqueeze(2)
                                  .to_broadcast([P, 2 * G, C]), ALU.mult).then_inc(v_scaled, 1)

            def finish(beta):
                H, b = beta // BH, beta % BH
                dve.wait_ge(av_done, beta + 1)
                dve.tensor_tensor(y_out[:, beta, :], ps[:, 6 + beta % 2, 0:NPIX],
                                  X[:, H, b * NPIX:(b + 1) * NPIX], ALU.add).then_inc(y_ready, 1)

            for H in range(HALVES):
                keys(H)
            for H in range(HALVES):
                values(H)
            for H in range(HALVES):
                for b in range(BH):
                    beta = H * BH + b
                    for n in (2 * beta, 2 * beta + 1):
                        dve.wait_ge(scores_done, n + 1)
                        bank = 2 * (n % DEEP)
                        dve.tensor_reduce(smin[:, n, :], ps[:, bank:bank + 2, :].rearrange(
                            "p n (t i) -> p (n t) i", t=2), AX_X, ALU.min).then_inc(max_ready, 1)
                    if beta >= 1:
                        scale_values(beta - 1)
                    if beta >= 2:
                        finish(beta - 2)
            last_beta = HALVES * BH - 1
            scale_values(last_beta)
            finish(last_beta - 1)
            finish(last_beta)


def kernel(x, L0_conv_ln1_w, L0_conv_ln2_w, L0_conv_dw_w, L0_conv_dw_b, L0_conv_qkvl_w, L0_conv_qkvl_b,
           L0_conv_fc1_w, L0_conv_fc1_b, L0_conv_pos_w, L0_conv_pos_b, L0_conv_fc2_w, L0_conv_fc2_b,
           L1_conv_Wq, L1_conv_bq, L1_conv_Wk, L1_conv_bk, L1_conv_Wv, L1_conv_bv):
    import numpy as np
    import concourse.bacc as bacc
    from concourse.bass_utils import run_bass_kernel_spmd

    f = np.float32

    def arr(a):
        return np.asarray(a)

    def tiled(a):
        return np.tile(arr(a).reshape(-1, 1), (G, 1))

    def blocks(w):
        w = arr(w)
        out = np.zeros((P, P), f)
        for g in range(G):
            out[C * g:C * (g + 1), C * g:C * (g + 1)] = w
        return out

    def diagonal(v):
        out = np.zeros((len(v), len(v)), f)
        out[np.arange(len(v)), np.arange(len(v))] = v
        return out

    slot = np.arange(P) % C
    centre = blocks(np.eye(C, dtype=f) - f(1) / f(C))
    ident = np.eye(P, dtype=f)
    mean = blocks(np.full((C, C), f(1) / f(C)))
    side2 = SIDE // 2
    pool = np.zeros((P, CLASSES, P), f)
    for cl in range(CLASSES):
        for half in range(2):
            for i in range(side2):
                for j in range(side2):
                    for a in ((i,) if cl // 2 == 0 else (i - 1, i)):
                        for b in ((j,) if cl % 2 == 0 else (j - 1, j)):
                            if a >= 0 and b >= 0:
                                pool[half * POOLED + a * side2 + b, cl, half * POOLED + i * side2 + j] = 1
    keep = diagonal((slot < C - C4).astype(f))
    is_v = (slot >= C - C4).astype(f).reshape(P, 1)
    minus_own = np.where(np.arange(P)[:, None] // C == np.arange(G)[None, :], f(-1), f(0)).astype(f)
    ones = np.zeros((P, P), f)
    ones[0] = 1

    dw = arr(L0_conv_dw_w).reshape(C2, 9)
    wall = arr(L0_conv_qkvl_w).reshape(4, C4, C2)
    ball = arr(L0_conv_qkvl_b).reshape(4, C4)
    taps = []
    for tap in ATTN_PE_TAPS:
        w = np.zeros((C, C), f)
        w[:C2, :C2] = diagonal(dw[:, tap])
        if tap == CENTRE:
            w[C2:, C2:C2 + C4] = wall[3].T
            w[C2:, C2 + C4:] = wall[2].T
        taps.append(blocks(w))
    attn_w = np.zeros((C, 9), f)
    attn_w[:C2] = dw
    attn_b = np.concatenate([arr(L0_conv_dw_b), ball[3], ball[2]])
    qk_w = np.zeros((P, 2, G, C4), f)
    qk_brow = np.zeros((P, 2, G, C4), f)
    for g in range(G):
        for which in range(2):
            qk_w[C * g + C2:C * (g + 1), which, g] = wall[which].T
            qk_brow[0, which, g] = ball[which]

    fc1 = arr(L0_conv_fc1_w).reshape(HID, C).T
    fc1_w = np.zeros((P, G, HID), f)
    for g in range(G):
        fc1_w[C * g:C * (g + 1), g] = fc1
    pos = arr(L0_conv_pos_w).reshape(HID, 9)

    def side_by_side(cols, n, **parts):
        out = np.zeros((P, n), f)
        for name, (a, b) in cols.items():
            out[:, a:b] = parts[name].reshape(P, b - a)
        return out

    first = side_by_side(FIRST_COLS, FIRST_N, centre=centre, ident=ident, mean=mean,
                         ln1_w=tiled(L0_conv_ln1_w), ln2_w=tiled(L0_conv_ln2_w))
    second = side_by_side(SECOND_COLS, SECOND_N, attn_taps=np.concatenate(taps, 1), attn_w=np.tile(attn_w, (G, 1)),
                          attn_b=tiled(attn_b), qk_w=qk_w, qk_brow=qk_brow, ones=ones, pool=pool, keep=keep,
                          is_v=is_v)
    third = side_by_side(THIRD_COLS, THIRD_N, fc1_w=fc1_w, fc1_b=arr(L0_conv_fc1_b),
                         mlp_taps=np.concatenate([diagonal(pos[:, t]) for t in range(9)], 1), pos_w=pos,
                         pos_b=arr(L0_conv_pos_b), fc2_w=arr(L0_conv_fc2_w).reshape(C, HID).T,
                         fc2_b=tiled(L0_conv_fc2_b), wq=blocks(arr(L1_conv_Wq).T), wk=blocks(arr(L1_conv_Wk).T),
                         wv=blocks(arr(L1_conv_Wv).T), bq=tiled(L1_conv_bq), bk=tiled(L1_conv_bk),
                         bv=np.broadcast_to(np.tile(arr(L1_conv_bv), G), (P, P)),
                         minus_own=minus_own)
    xs = arr(x).reshape(G, HALVES, BH, C, SIDE, SIDE).transpose(0, 3, 1, 4, 2, 5).reshape(P, HALVES * COLS)

    nc = bacc.Bacc("TRN2", target_bir_lowering=False, num_devices=1)
    arrays = {"x_in": np.ascontiguousarray(xs), "first_in": first, "second_in": second, "third_in": third}
    args = [nc.dram_tensor(n, a.shape, F32, kind="ExternalInput").ap() for n, a in arrays.items()]
    args.append(nc.dram_tensor("y", (P, HALVES * COLS), F32, kind="ExternalOutput").ap())
    build(nc, *args)
    r = run_bass_kernel_spmd(nc, [arrays], core_ids=[0])
    y = np.asarray(r.results[0]["y"]).reshape(G, C, HALVES, BH, SIDE, SIDE)
    return y.transpose(0, 2, 3, 1, 4, 5).reshape(B, C, SIDE, SIDE)
```

```python
from contextlib import ExitStack

import concourse.bass as bass
from concourse import mybir

ALU = mybir.AluOpType
ACT = mybir.ActivationFunctionType
F32 = mybir.dt.float32
AX_X = mybir.AxisListType.X

P = 128
C = 32
G = P // C
B = 32
SIDE = 16
NPIX = SIDE * SIDE
HALVES = 2
BH = B // G // HALVES
COLS = BH * NPIX
BANK = 512
NB = COLS // BANK
C2, C4 = C // 2, C // 4
HID = 128
ROW = SIDE + 1
PROWS = (SIDE + 2) * BH + 1
PADDED = PROWS * ROW
INNER = BH * ROW + 1
ROWS = SIDE * BH
PAIRS = BH // 2
CLASSES = 4
POOLED = NPIX // 4
UNITS = BH * G
TILES = HALVES * G
BATCH_ORDER = [0, 2, 1, 3]
LN_EPS = 1e-5

TAPS = [(dy, dx) for dy in (-1, 0, 1) for dx in (-1, 0, 1)]
CENTRE = 4
ATTN_TAP_ORDER = [4, 0, 1, 2, 3, 5, 6, 7, 8]
ATTN_PE_TAPS = 3
ATTN_DVE_TAPS = len(ATTN_TAP_ORDER) - ATTN_PE_TAPS
ATTN_STEPS = NB * ATTN_PE_TAPS
MLP_PE_TAPS = [1, 2, 2, 3, 2, 3, 2, 5]
MLP_POOL_TAPS = [1, 2, 2, 1, 1, 1, 0, 0]
LAST_DVE_TAP = [8 - n for n in MLP_POOL_TAPS]
PRODUCTS = [(i, tap) for i in range(TILES) for tap in range(LAST_DVE_TAP[i] + 1, 9)]
PRODUCT_SLOTS = 4


def mlp_tap_order():
    order, tail = [], []
    for i in range(TILES):
        own = [(i, tap) for tap in range(MLP_PE_TAPS[i], LAST_DVE_TAP[i] + 1)]
        lead = own[:len(own) // 2]
        for j in range(max(len(tail), len(lead))):
            order += tail[j:j + 1] + lead[j:j + 1]
        tail = own[len(own) // 2:]
    return order + tail


TAP_ORDER = mlp_tap_order()
TAPS_DONE = {at: n + 1 for n, at in enumerate(TAP_ORDER)}
FIRST_HALF_DONE = TAPS_DONE[3, LAST_DVE_TAP[3]]
DVE_AT = {"m1": TAPS_DONE[0, LAST_DVE_TAP[0]], "X0": FIRST_HALF_DONE + 4, "keys0": FIRST_HALF_DONE + 6,
          "values0": FIRST_HALF_DONE + 8}
TAPS_AFTER_UNIT = [1, 1, 2, 1, 0, 2, 0, 0, 1, 0, 1, 3]
CONV7_STEPS = 2
AV_LAG = 9


def columns(sizes):
    at, out = 0, {}
    for name, n in sizes:
        out[name] = (at, at + n)
        at += n
    return out, at


FIRST_COLS, FIRST_N = columns([("centre", P), ("ident", P), ("mean", P), ("ln1_w", 1), ("ln2_w", 1)])
SECOND_COLS, SECOND_N = columns([
    ("attn_w", 9), ("attn_b", 1), ("qk_w", 2 * G * C4),
    ("qk_brow", 2 * G * C4), ("ones", P), ("pool", CLASSES * P), ("keep", P), ("is_v", 1),
    ("attn_taps", ATTN_PE_TAPS * P),
])
THIRD_COLS, THIRD_N = columns([
    ("fc1_w", G * HID), ("fc1_b", 1), ("mlp_taps", P * 9), ("pos_w", 9), ("pos_b", 1),
    ("fc2_w", C), ("fc2_b", 1), ("wq", P), ("wk", P), ("wv", P), ("bq", 1), ("bk", 1), ("bv", P),
    ("minus_own", G),
])


def build(nc, x_in, first_in, second_in, third_in, out):
    with ExitStack() as ctx:
        def sb(name, shape):
            return ctx.enter_context(nc.sbuf_tensor(name, shape, F32))

        def sem(name):
            return ctx.enter_context(nc.semaphore(name))

        def half_sems(name):
            return [sem(f"{name}{H}") for H in range(HALVES)]

        ps = ctx.enter_context(nc.psum_tensor("ps", [P, 8, BANK], F32))

        x = sb("x", [P, HALVES, COLS])
        first = sb("first", [P, FIRST_N])
        second = sb("second", [P, SECOND_N])
        third = sb("third", [P, THIRD_N])
        padded = sb("padded", [P, HALVES * (1 + G), PADDED])
        acc = sb("acc", [P, TILES, COLS])
        product = sb("product", [P, PRODUCT_SLOTS, COLS])
        eps_col = sb("eps_col", [P, 1])
        qk_tok = sb("qk_tok", [P, HALVES, PAIRS * CLASSES * 2 * G * C4])
        kf = sb("kf", [P, HALVES, PAIRS, P])
        qf = sb("qf", [P, HALVES, PAIRS, G * C4])
        att = sb("att", [P, HALVES, BH, C4])
        att_max = sb("att_max", [P, HALVES, BH])
        att_sum = sb("att_sum", [P, HALVES, BH])
        att_inv = sb("att_inv", [P, HALVES, BH])
        att_blocks = sb("att_blocks", [P, HALVES, BH, P])
        mix_w = sb("mix_w", [P, HALVES, BH, P])
        res1 = sb("res1", [P, HALVES, COLS])
        skip = sb("skip", [P, HALVES, COLS])
        m = sb("m", [P, HALVES, COLS])
        X = sb("X", [P, HALVES, COLS])
        v_tok = sb("v_tok", [P, HALVES * BH, 2, G, C])
        prob = sb("prob", [P, 2, G, 2, NPIX])
        k_bias = sb("k_bias", [P, G])
        smin = sb("smin", [P, HALVES * UNITS, 2])
        psum_row = sb("psum_row", [P, HALVES * BH, 2, G])
        inv_row = sb("inv_row", [P, HALVES * BH, 2, G])
        y_out = sb("y_out", [P, HALVES * BH, NPIX])

        def attn_acc(H):
            return acc[:, G * H, :]

        def squares(H):
            return acc[:, G * H + 1, :]

        def rstd(H):
            return acc[:, G * H + 2, :]

        def norm_parity(H):
            return acc[:, G * H + 3, :].rearrange("p (k n) -> p k n", k=CLASSES)

        def k_split(H):
            lo = HALVES + G * H
            return padded[:, lo:lo + G, :].rearrange("p n c -> p (n c)")[:, 0:G * COLS].rearrange(
                "p (g c) -> p g c", g=G)

        def cols(n):
            return slice(n * BANK, (n + 1) * BANK)

        def c1(name):
            return first[:, FIRST_COLS[name][0]:FIRST_COLS[name][1]]

        def c2(name):
            return second[:, SECOND_COLS[name][0]:SECOND_COLS[name][1]]

        def c3(name):
            return third[:, THIRD_COLS[name][0]:THIRD_COLS[name][1]]

        def big(H):
            return ps[:, 4 * H:4 * H + NB, :]

        def conv_banks(H):
            return ps[:, 4 * H + NB:4 * H + 2 * NB, :]

        def small(H, which):
            return ps[:, 4 * H + NB + which, :]

        def flat(banks):
            return banks.rearrange("p n c -> p (n c)")

        def tap_view(buf, tap, bank=None):
            dy, dx = TAPS[tap]
            off = INNER + dy * BH * ROW + dx
            n = ROWS if bank is None else ROWS // NB
            off += 0 if bank is None else bank * n * ROW
            return padded[:, buf, off:off + n * ROW].rearrange("p (r s) -> p r s", s=ROW)[:, :, 0:SIDE]

        def rows(ap):
            return ap.rearrange("p (r s) -> p r s", s=SIDE)

        def by_batch(ap):
            return ap.rearrange("p (y b s) -> p b y s", b=BH, s=SIDE)

        score_banks = ((0, 1, 2), (4, 5, 6, 0, 1, 2))

        def score_bank(H, u):
            return score_banks[H][u % len(score_banks[H])]

        def av_bank(H, b):
            return 3 if H == 0 else (7, 3)[b % 2]

        x_loaded = [[sem(f"x_loaded{H}{n}") for n in range(NB)] for H in range(HALVES)]
        first_loaded, second_loaded, third_loaded = sem("first_loaded"), sem("second_loaded"), sem("third_loaded")
        eps_set, attn_border_zeroed, kf_zeroed, blocks_zeroed, mlp_border_zeroed = (
            sem("eps_set"), sem("attn_border_zeroed"), sem("kf_zeroed"), sem("blocks_zeroed"),
            sem("mlp_border_zeroed"))
        centred, squared, var_ready, log_ready, rstd_ready, normed = (
            half_sems("centred"), half_sems("squared"), half_sems("var_ready"), half_sems("log_ready"),
            half_sems("rstd_ready"), half_sems("normed"))
        parity_split, qk_proj, qk_gelu, k_pooled, q_pooled, q_scaled = (
            half_sems("parity_split"), half_sems("qk_proj"), half_sems("qk_gelu"), half_sems("k_pooled"),
            half_sems("q_pooled"), half_sems("q_scaled"))
        att_scores, att_exp_in, att_exp, att_placed, att_turned, mix_ready = (
            half_sems("att_scores"), half_sems("att_exp_in"), half_sems("att_exp"), half_sems("att_placed"),
            half_sems("att_turned"), half_sems("mix_ready"))
        attn_conv_pe, attn_gelu, mixed, res1_ready = (
            half_sems("attn_conv_pe"), half_sems("attn_gelu"), half_sems("mixed"), half_sems("res1_ready"))
        attn_sum, skip_ready = half_sems("attn_sum"), half_sems("skip_ready")
        fc1_done, hid_gelu, conv_pe, conv_sum, conv_gelu = (
            sem("fc1_done"), sem("hid_gelu"), sem("conv_pe"), sem("conv_sum"), sem("conv_gelu"))
        product_ready, pool_sum = sem("product_ready"), sem("pool_sum")
        fc2_done, X_ready = half_sems("fc2_done"), half_sems("X_ready")
        q_proj, q_ready, k_proj, k_low_ready, k_ready, v_proj, v_ready = (
            half_sems("q_proj"), half_sems("q_ready"), half_sems("k_proj"), half_sems("k_low_ready"),
            half_sems("k_ready"), half_sems("v_proj"), half_sems("v_ready"))
        k_bias_ready = sem("k_bias_ready")
        scores_done, min_ready, exp_done, v_scaled, av_done, y_ready, stored = (
            sem("scores_done"), sem("min_ready"), sem("exp_done"), sem("v_scaled"), sem("av_done"),
            sem("y_ready"), sem("stored"))
        dve_chain = sem("dve_chain")

        block = ctx.enter_context(nc.Block())

        @block.sync
        def _(sp):
            for H in range(HALVES):
                for n in range(NB):
                    at = H * COLS + n * BANK
                    sp.dma_start(x[:, H, cols(n)], x_in[:, at:at + BANK]).then_inc(x_loaded[H][n], 16)
            sp.dma_start(second[:, :], second_in).then_inc(second_loaded, 16)
            sp.dma_start(third[:, :], third_in).then_inc(third_loaded, 16)
            for beta in range(HALVES * BH):
                sp.wait_ge(y_ready, beta + 1)
                sp.dma_start(out[:, beta * NPIX:(beta + 1) * NPIX], y_out[:, beta, :]).then_inc(stored, 16)
            sp.wait_ge(stored, 16 * HALVES * BH)

        @block.gpsimd
        def _(pool):
            def zero_border(lo, hi, zeroed):
                tiles = padded[:, lo:hi, :]
                last_rows = (PROWS - 1 - BH) * ROW
                pool.memset(tiles[:, :, 0:BH * ROW], 0.0).then_inc(zeroed, 1)
                pool.memset(tiles[:, :, last_rows:PADDED], 0.0).then_inc(zeroed, 1)
                pool.memset(tiles[:, :, BH * ROW:last_rows].rearrange("p n (r s) -> p n r s", s=ROW)[:, :, :, 0:1],
                            0.0).then_inc(zeroed, 1)

            pool.memset(eps_col[:, :], LN_EPS).then_inc(eps_set, 1)
            zero_border(0, HALVES, attn_border_zeroed)
            pool.memset(kf[:, :, :, :], 0.0).then_inc(kf_zeroed, 1)
            pool.memset(att_blocks[:, :, :, :], 0.0).then_inc(blocks_zeroed, 1)
            zero_border(HALVES, HALVES + TILES, mlp_border_zeroed)
            pool.wait_ge(third_loaded, 16)
            for H in range(HALVES):
                pool.wait_ge(res1_ready[H], NB)
                pool.tensor_scalar(skip[:, H, :], res1[:, H, :], c3("fc2_b"), None, ALU.add).then_inc(skip_ready[H], 1)
            for n, (i, tap) in enumerate(PRODUCTS):
                pool.wait_ge(product_ready, n + 1)
                pool.wait_ge(conv_sum, TAPS_DONE[i, LAST_DVE_TAP[i]])
                if n >= 1:
                    pool.wait_ge(pool_sum, n)
                pool.tensor_tensor(acc[:, i, :], acc[:, i, :], product[:, n % PRODUCT_SLOTS, :], ALU.add
                                   ).then_inc(pool_sum, 1)

        @block.tensor
        def _(pe):
            def centre(H):
                for n in range(NB):
                    pe.wait_ge(x_loaded[H][n], 16)
                    pe.matmul(big(H)[:, n, :], c1("centre"), x[:, H, cols(n)],
                              start=True, stop=True).then_inc(centred[H], 1)

            def variance(ln, H):
                for n in range(NB):
                    pe.wait_ge(squared[H], NB * ln + n + 1)
                    pe.matmul(big(H)[:, n, :], c1("mean"), squares(H)[:, cols(n)],
                              start=True, stop=True).then_inc(var_ready[H], 1)

            def qk(H):
                pe.wait_ge(parity_split[H], 1)
                pe.matmul(small(H, 0), c2("ones")[0:1, :],
                          c2("qk_brow")[0:1, :].unsqueeze(1).to_broadcast([1, PAIRS * CLASSES, 2 * G * C4]),
                          start=True, stop=False)
                for pair in range(PAIRS):
                    for cl in range(CLASSES):
                        at = (pair * CLASSES + cl) * 2 * G * C4
                        last = pe.matmul(small(H, 0)[:, at:at + 2 * G * C4],
                                         norm_parity(H)[:, cl, pair * P:(pair + 1) * P],
                                         c2("qk_w"), start=False, stop=(pair, cl) == (PAIRS - 1, CLASSES - 1))
                last.then_inc(qk_proj[H], 1)

            def attn_conv(H, first_step, last_step):
                pe.wait_ge(normed[H], NB)
                for step in range(first_step, last_step):
                    n, i = step // ATTN_PE_TAPS, step % ATTN_PE_TAPS
                    last = pe.matmul(big(H)[:, n, :], c2("attn_taps")[:, i * P:(i + 1) * P],
                                     tap_view(H, ATTN_TAP_ORDER[i], n), start=i == 0, stop=i == ATTN_PE_TAPS - 1)
                if last_step == ATTN_STEPS:
                    last.then_inc(attn_conv_pe[H], 1)

            def pool_queries(H):
                pe.wait_ge(qk_gelu[H], 1)
                q_cols = qk_tok[:, H, :].rearrange("p (a k w d) -> p a k w d", a=PAIRS, k=CLASSES, w=2)
                for cl in range(CLASSES):
                    last = pe.matmul(small(H, 1)[:, 64:64 + PAIRS * G * C4], c2("pool")[:, cl * P:(cl + 1) * P],
                                     q_cols[:, :, cl, 0, :], start=cl == 0, stop=cl == CLASSES - 1)
                last.then_inc(q_pooled[H], 1)

            def channel_scores(H):
                pe.wait_ge(k_pooled[H], 1)
                pe.wait_ge(q_scaled[H], 1)
                for b in BATCH_ORDER:
                    pair, half = b // 2, b % 2
                    lo = POOLED * half
                    last = pe.matmul(small(H, half)[:, 128 + pair * G * C4:128 + (pair + 1) * G * C4],
                                     kf[lo:lo + POOLED, H, pair, :], qf[lo:lo + POOLED, H, pair, :],
                                     start=True, stop=True)
                last.then_inc(att_scores[H], 1)

            def turn(H):
                pe.wait_ge(att_placed[H], 1)
                for b in range(BH):
                    last = pe.transpose(small(H, 0)[:, b * P:(b + 1) * P], att_blocks[:, H, b, :], c1("ident"))
                last.then_inc(att_turned[H], 1)

            def mix(H):
                pe.wait_ge(mix_ready[H], 1)
                pe.wait_ge(attn_gelu[H], 1)
                for b in range(BH):
                    at = b * NPIX
                    last = pe.matmul(big(H)[:, at // BANK, at % BANK:at % BANK + NPIX],
                                     mix_w[:, H, BATCH_ORDER.index(b), :],
                                     by_batch(attn_acc(H))[:, b, :, :], start=True, stop=True)
                    if (at + NPIX) % BANK == 0:
                        last.then_inc(mixed[H], 1)

            def centre2(H):
                for n in range(NB):
                    pe.wait_ge(res1_ready[H], n + 1)
                    pe.matmul(big(H)[:, n, :], c1("centre"), res1[:, H, cols(n)],
                              start=True, stop=True).then_inc(centred[H], 1)

            def fc1(i):
                H, g = i // G, i % G
                if g == 0:
                    pe.wait_ge(normed[H], 2 * NB)
                else:
                    pe.wait_ge(hid_gelu, i)
                w = c3("fc1_w")[:, g * HID:(g + 1) * HID]
                m_rows = m[:, H, :].rearrange("p (b y s) -> p y b s", b=BH, s=SIDE)
                for n in range(NB):
                    last = pe.matmul(big(H)[:, n, :], w, m_rows[:, SIDE // NB * n:SIDE // NB * (n + 1), :, :],
                                     start=True, stop=True)
                last.then_inc(fc1_done, 1)

            def conv(i, first_step=0, last_step=None):
                H, g = i // G, i % G
                n_taps = MLP_PE_TAPS[i]
                last_step = NB * n_taps if last_step is None else min(last_step, NB * n_taps)
                if first_step == 0:
                    pe.wait_ge(hid_gelu, i + 1)
                    if g >= 1:
                        pe.wait_ge(conv_sum, TAPS_DONE[i - 1, MLP_PE_TAPS[i - 1]])
                for step in range(first_step, last_step):
                    n, tap = step // n_taps, step % n_taps
                    last = pe.matmul(conv_banks(H)[:, n, :], c3("mlp_taps")[:, tap * P:(tap + 1) * P],
                                     tap_view(HALVES + i, tap, n), start=tap == 0, stop=tap == n_taps - 1)
                if first_step < last_step == NB * n_taps:
                    last.then_inc(conv_pe, 1)

            def fc2_part(H, part):
                for n in range(NB):
                    for g in range(G):
                        i = G * H + g
                        if n == 0 and part == 0:
                            pe.wait_ge(hid_gelu, i + 1)
                        if n == 0 and part == 1:
                            pe.wait_ge(conv_gelu, i + 1)
                        h = padded[:, HALVES + i, INNER:INNER + ROWS * ROW].rearrange(
                            "p (y b s) -> p b y s", b=BH, s=ROW)[:, :, :, 0:SIDE]
                        rhs = (h, by_batch(acc[:, i, :]))[part][:, BH // NB * n:BH // NB * (n + 1), :, :]
                        last = pe.matmul(big(H)[C * g:C * (g + 1), n, :], c3("fc2_w"), rhs,
                                         start=part == 0, stop=part == 1)
                    if part == 1:
                        last.then_inc(fc2_done[H], 1)

            def queries_and_keys(H):
                for n in range(NB):
                    pe.wait_ge(X_ready[H], n + 1)
                    pe.matmul(conv_banks(H)[:, n, :], c3("wk"), X[:, H, cols(n)],
                              start=True, stop=True).then_inc(k_proj[H], 1)
                    pe.matmul(big(H)[:, n, :], c3("wq"), X[:, H, cols(n)],
                              start=True, stop=True).then_inc(q_proj[H], 1)

            def values(H):
                if H == 0:
                    pe.wait_ge(q_ready[0], NB)
                else:
                    pe.wait_ge(exp_done, UNITS)
                for b in range(BH):
                    for jt in range(2):
                        at = (2 * b + jt) * P
                        last = pe.matmul(ps[:, at // BANK, at % BANK:at % BANK + P],
                                         X[:, H, at:at + P], c3("wv"),
                                         start=True, stop=True)
                last.then_inc(v_proj[H], 1)

            def scores(H, u):
                b, g = u // G, u % G
                ahead = len(score_banks[H])
                if u % (UNITS // NB) == 0:
                    pe.wait_ge(q_ready[H], u // (UNITS // NB) + 1)
                    pe.wait_ge(k_ready[H], u // (UNITS // NB) + 1)
                if u == 0 and H == 0:
                    pe.wait_ge(v_ready[0], 1)
                if u == 1:
                    pe.wait_ge(q_ready[H], NB)
                if H == 1 and u == 3:
                    pe.wait_ge(v_ready[1], 1)
                if u >= ahead:
                    pe.wait_ge(exp_done, UNITS * H + u - ahead + 1)
                for jt in range(2):
                    at = b * NPIX + jt * P
                    last = pe.matmul(ps[:, score_bank(H, u), jt * NPIX:(jt + 1) * NPIX],
                                     k_split(H)[:, g, at:at + P], m[:, H, b * NPIX:(b + 1) * NPIX],
                                     start=True, stop=True)
                last.then_inc(scores_done, 1)

            def weighted_values(H, b):
                beta = BH * H + b
                pe.wait_ge(v_scaled, beta + 1)
                if b == 0:
                    pe.wait_ge(k_ready[H], NB)
                if beta > 0 and (H, b) != (1, 0):
                    pe.wait_ge(y_ready, beta if H == 0 else max(BH, beta - 1))
                for jt in range(2):
                    for g in range(G):
                        last = pe.matmul(ps[C * g:C * (g + 1), av_bank(H, b), 0:NPIX], v_tok[:, beta, jt, g, :],
                                         prob[:, beta % 2, g, jt, :], start=jt == 0, stop=jt == 1)
                last.then_inc(av_done, 1)

            pe.wait_ge(first_loaded, 16)
            for H in range(HALVES):
                centre(H)
                variance(0, H)
            pe.wait_ge(second_loaded, 16)
            pe.wait_ge(attn_border_zeroed, 3)
            attn_conv(0, 0, 2)
            qk(0)
            attn_conv(0, 2, 3)
            pool_queries(0)
            attn_conv(0, 3, 4)
            pe.wait_ge(kf_zeroed, 1)
            channel_scores(0)
            attn_conv(0, 4, ATTN_STEPS)
            qk(1)
            pe.wait_ge(blocks_zeroed, 1)
            turn(0)
            attn_conv(1, 0, 2)
            pool_queries(1)
            mix(0)
            attn_conv(1, 2, 5)
            channel_scores(1)
            centre2(0)
            attn_conv(1, 5, ATTN_STEPS)
            variance(1, 0)
            turn(1)
            pe.wait_ge(third_loaded, 16)
            pe.wait_ge(mlp_border_zeroed, 3)
            fc1(0)
            mix(1)
            conv(0)
            fc1(1)
            centre2(1)
            conv(1)
            fc1(2)
            variance(1, 1)
            conv(2)
            fc1(3)
            fc1(4)
            conv(3)
            fc1(5)
            conv(4)
            fc1(6)
            fc2_part(0, 0)
            conv(5)
            fc2_part(0, 1)
            queries_and_keys(0)
            conv(6, 0, MLP_PE_TAPS[6])
            values(0)
            conv(6, MLP_PE_TAPS[6])
            fc1(7)
            for u in range(UNITS - G):
                scores(0, u)
                if u >= 1:
                    conv(7, (u - 1) * CONV7_STEPS, u * CONV7_STEPS)
                if u >= 6 and u % G == 2:
                    weighted_values(0, (u - 6) // G)
            conv(7, (UNITS - G - 1) * CONV7_STEPS)
            fc2_part(1, 0)
            for u in range(UNITS - G, UNITS - 1):
                scores(0, u)
            fc2_part(1, 1)
            weighted_values(0, BH - 2)
            scores(0, UNITS - 1)
            queries_and_keys(1)
            values(1)
            for u in range(UNITS):
                scores(1, u)
                if u == 1:
                    weighted_values(0, BH - 1)
                if u >= AV_LAG and (u - AV_LAG) % G == 0:
                    weighted_values(1, (u - AV_LAG) // G)
            for b in range((UNITS - 1 - AV_LAG) // G + 1, BH):
                weighted_values(1, b)

        @block.scalar
        def _(act):
            def square(ln, H):
                for n in range(NB):
                    act.wait_ge(centred[H], NB * ln + n + 1)
                    act.activation(squares(H)[:, cols(n)], big(H)[:, n, :], ACT.Square).then_inc(squared[H], 1)

            def inverse_root(ln, H):
                for n in range(NB):
                    act.wait_ge(var_ready[H], NB * ln + n + 1)
                    act.activation(rstd(H)[:, cols(n)], big(H)[:, n, :], ACT.Ln, bias=eps_col[:, :]
                                   ).then_inc(log_ready[H], 1)
                    act.wait_ge(log_ready[H], NB * ln + n + 1)
                    act.activation(rstd(H)[:, cols(n)], rstd(H)[:, cols(n)], ACT.Exp, scale=-0.5
                                   ).then_inc(rstd_ready[H], 1)

            def split_parities(H):
                act.wait_ge(normed[H], NB)
                whole = padded[:, H, INNER:INNER + ROWS * ROW].rearrange("p (y b s) -> p b y s", b=BH, s=ROW)
                for cl in range(CLASSES):
                    last = act.activation(
                        norm_parity(H)[:, cl, :].rearrange("p (b i j) -> p b i j", b=BH, j=SIDE // 2),
                        whole[:, :, cl // 2::2, cl % 2:SIDE:2], ACT.Copy)
                last.then_inc(parity_split[H], 1)

            def qk_act(H):
                act.wait_ge(qk_proj[H], 1)
                act.activation(qk_tok[:, H, :], small(H, 0), ACT.Gelu).then_inc(qk_gelu[H], 1)

            def scale_queries(H):
                act.wait_ge(q_pooled[H], 1)
                act.activation(qf[:, H, :, :].rearrange("p a d -> p (a d)"),
                               small(H, 1)[:, 64:64 + PAIRS * G * C4], ACT.Copy, scale=1.0 / 9.0
                               ).then_inc(q_scaled[H], 1)

            def channel_exp(H):
                act.wait_ge(att_exp_in[H], 1)
                act.activation(att[:, H, :, :], att[:, H, :, :], ACT.Exp).then_inc(att_exp[H], 1)

            def attn_act(H):
                act.wait_ge(second_loaded, 16)
                act.wait_ge(attn_sum[H], ATTN_DVE_TAPS + 1)
                act.activation(attn_acc(H), attn_acc(H), ACT.Gelu, bias=c2("attn_b")).then_inc(attn_gelu[H], 1)

            def hidden(i):
                act.wait_ge(fc1_done, i + 1)
                act.activation(tap_view(HALVES + i, CENTRE), rows(flat(big(i // G))),
                               ACT.Gelu, bias=c3("fc1_b")).then_inc(hid_gelu, 1)

            def products(i):
                for tap in range(LAST_DVE_TAP[i] + 1, 9):
                    n = PRODUCTS.index((i, tap))
                    act.wait_ge(hid_gelu, i + 1)
                    if n >= PRODUCT_SLOTS:
                        act.wait_ge(pool_sum, n - PRODUCT_SLOTS + 1)
                    act.activation(rows(product[:, n % PRODUCT_SLOTS, :]), tap_view(HALVES + i, tap), ACT.Copy,
                                   scale=c3("pos_w")[:, tap:tap + 1]).then_inc(product_ready, 1)

            def conv_act(i):
                if MLP_POOL_TAPS[i]:
                    act.wait_ge(pool_sum, PRODUCTS.index((i, 8)) + 1)
                else:
                    act.wait_ge(conv_sum, TAPS_DONE[i, 8])
                act.activation(acc[:, i, :], acc[:, i, :], ACT.Gelu, bias=c3("pos_b")).then_inc(conv_gelu, 1)

            def queries_and_high_keys(H):
                act.wait_ge(k_bias_ready, 1)
                for n in range(NB):
                    act.wait_ge(q_proj[H], n + 1)
                    act.activation(m[:, H, cols(n)], big(H)[:, n, :], ACT.Identity, bias=c3("bq")
                                   ).then_inc(q_ready[H], 1)
                    act.wait_ge(k_low_ready[H], n + 1)
                    for g in range(2, G):
                        last = act.activation(k_split(H)[:, g, cols(n)], conv_banks(H)[:, n, :], ACT.Identity,
                                              scale=c3("minus_own")[:, g:g + 1], bias=k_bias[:, g:g + 1])
                    last.then_inc(k_ready[H], 1)

            def pixel_exp(H, units):
                for u in units:
                    b, g = u // G, u % G
                    beta, unit = BH * H + b, UNITS * H + u
                    act.wait_ge(min_ready, unit + 1)
                    if g == 0 and beta >= 2:
                        act.wait_ge(av_done, beta - 1)
                    for jt in range(2):
                        last = act.activation(prob[:, beta % 2, g, jt, :],
                                              ps[:, score_bank(H, u), jt * NPIX:(jt + 1) * NPIX],
                                              ACT.Exp, scale=-1.0, bias=smin[:, unit, jt:jt + 1],
                                              accum_out=psum_row[:, beta, jt, g:g + 1])
                    last.then_inc(exp_done, 1)

            act.dma_start(first[:, :], first_in).then_inc(first_loaded, 16)
            act.preload_act_table_set("natural_log_exp_and_others")
            act.wait_ge(eps_set, 1)
            square(0, 0)
            inverse_root(0, 0)
            square(0, 1)
            split_parities(0)
            inverse_root(0, 1)
            split_parities(1)
            act.preload_act_table_set("gelu_and_others")
            qk_act(0)
            scale_queries(0)
            act.preload_act_table_set("natural_log_exp_and_others")
            channel_exp(0)
            act.preload_act_table_set("gelu_and_others")
            qk_act(1)
            attn_act(0)
            scale_queries(1)
            act.preload_act_table_set("natural_log_exp_and_others")
            square(1, 0)
            channel_exp(1)
            inverse_root(1, 0)
            act.preload_act_table_set("gelu_and_others")
            attn_act(1)
            act.wait_ge(third_loaded, 16)
            hidden(0)
            hidden(1)
            square(1, 1)
            products(0)
            hidden(2)
            products(1)
            act.preload_act_table_set("natural_log_exp_and_others")
            inverse_root(1, 1)
            act.preload_act_table_set("gelu_and_others")
            conv_act(0)
            hidden(3)
            products(2)
            hidden(4)
            products(3)
            conv_act(1)
            hidden(5)
            products(4)
            conv_act(2)
            hidden(6)
            products(5)
            conv_act(3)
            queries_and_high_keys(0)
            hidden(7)
            products(6)
            products(7)
            conv_act(4)
            act.preload_act_table_set("natural_log_exp_and_others")
            pixel_exp(0, range(UNITS - G))
            act.preload_act_table_set("gelu_and_others")
            conv_act(5)
            conv_act(6)
            conv_act(7)
            act.preload_act_table_set("natural_log_exp_and_others")
            pixel_exp(0, range(UNITS - G, UNITS))
            queries_and_high_keys(1)
            pixel_exp(1, range(UNITS))

        @block.vector
        def _(dve):
            count = [0]

            def link(ins):
                count[0] += 1
                ins.then_inc(dve_chain, 1)
                dve.wait_ge(dve_chain, count[0])

            def attn_taps(H, js):
                for j in js:
                    tap = ATTN_TAP_ORDER[ATTN_PE_TAPS + j]
                    w = c2("attn_w")[:, tap:tap + 1]
                    if j == 0:
                        dve.wait_ge(normed[H], NB)
                        dve.tensor_scalar(rows(attn_acc(H)), tap_view(H, tap), w, None, ALU.mult
                                          ).then_inc(attn_sum[H], 1)
                    else:
                        dve.wait_ge(attn_sum[H], j)
                        dve.scalar_tensor_tensor(out=rows(attn_acc(H)), in0=tap_view(H, tap), scalar=w,
                                                 in1=rows(attn_acc(H)), op0=ALU.mult, op1=ALU.add
                                                 ).then_inc(attn_sum[H], 1)

            def add_pe_taps(H):
                dve.wait_ge(attn_conv_pe[H], 1)
                dve.wait_ge(attn_sum[H], ATTN_DVE_TAPS)
                dve.tensor_tensor(attn_acc(H), attn_acc(H), flat(big(H)), ALU.add).then_inc(attn_sum[H], 1)

            def pool_keys(H):
                dve.wait_ge(qk_gelu[H], 1)
                k_cols = qk_tok[:, H, :].rearrange("p (a k w g d) -> p a w g d k", a=PAIRS, k=CLASSES, w=2, g=G)
                for pair in range(PAIRS):
                    ins = dve.tensor_reduce(
                        kf[:, H, pair, :].rearrange("p (g s) -> p g s", g=G)[:, :, C - C4:C],
                        k_cols[:, pair, 1, :, :, :], AX_X, ALU.max)
                ins.then_inc(k_pooled[H], 1)

            def softmax_in(H):
                dve.wait_ge(att_scores[H], 1)
                blocks = conv_banks(H)[:, :, 128:128 + PAIRS * G * C4].rearrange(
                    "p h (a g d) -> p h a g d", a=PAIRS, g=G)
                for g in range(G):
                    ins = dve.tensor_copy(
                        att[C * g:C * (g + 1), H, :, :].rearrange("p (h a) d -> p h a d", h=2),
                        blocks[C * g:C * (g + 1), :, :, g, :])
                link(ins)
                link(dve.tensor_reduce(att_max[:, H, :], att[:, H, :, :], AX_X, ALU.max))
                dve.tensor_tensor(att[:, H, :, :], att[:, H, :, :],
                                  att_max[:, H, :].unsqueeze(2).to_broadcast([P, BH, C4]), ALU.subtract
                                  ).then_inc(att_exp_in[H], 1)

            def softmax_out(H):
                dve.wait_ge(att_exp[H], 1)
                link(dve.tensor_reduce(att_sum[:, H, :], att[:, H, :, :], AX_X, ALU.add))
                link(dve.reciprocal(att_inv[:, H, :], att_sum[:, H, :]))
                link(dve.tensor_scalar(att_inv[:, H, :], att_inv[:, H, :], c2("is_v"), None, ALU.mult))
                for g in range(G):
                    sl = slice(C * g, C * (g + 1))
                    ins = dve.tensor_tensor(att_blocks[sl, H, :, C * (g + 1) - C4:C * (g + 1)], att[sl, H, :, :],
                                            att_inv[sl, H, :].unsqueeze(2).to_broadcast([C, BH, C4]), ALU.mult)
                ins.then_inc(att_placed[H], 1)

            def mix_weights(H):
                dve.wait_ge(att_turned[H], 1)
                dve.tensor_tensor(mix_w[:, H, :, :], small(H, 0).rearrange("p (b c) -> p b c", b=BH),
                                  c2("keep").unsqueeze(1).to_broadcast([P, BH, P]), ALU.add
                                  ).then_inc(mix_ready[H], 1)

            def residual(H):
                for n in range(NB):
                    batches = slice(BH // NB * n, BH // NB * (n + 1))
                    dve.wait_ge(mixed[H], n + 1)
                    dve.tensor_tensor(res1[:, H, cols(n)].rearrange("p (b y s) -> p b y s", y=SIDE, s=SIDE),
                                      big(H)[:, n, :].rearrange("p (b y s) -> p b y s", y=SIDE, s=SIDE),
                                      by_batch(x[:, H, :])[:, batches, :, :], ALU.add).then_inc(res1_ready[H], 1)

            def normalise(H):
                for n in range(NB):
                    dve.wait_ge(rstd_ready[H], NB + n + 1)
                    dve.wait_ge(res1_ready[H], n + 1)
                    dve.scalar_tensor_tensor(out=m[:, H, cols(n)], in0=res1[:, H, cols(n)], scalar=c1("ln2_w"),
                                             in1=rstd(H)[:, cols(n)], op0=ALU.mult, op1=ALU.mult
                                             ).then_inc(normed[H], 1)

            def conv_taps(first_step, last_step):
                for i, tap in TAP_ORDER[first_step:last_step]:
                    if tap == MLP_PE_TAPS[i]:
                        dve.wait_ge(conv_pe, i + 1)
                        so_far = flat(conv_banks(i // G))
                    else:
                        dve.wait_ge(conv_sum, TAPS_DONE[i, tap - 1])
                        so_far = acc[:, i, :]
                    dve.scalar_tensor_tensor(out=rows(acc[:, i, :]), in0=tap_view(HALVES + i, tap),
                                             scalar=c3("pos_w")[:, tap:tap + 1], in1=rows(so_far),
                                             op0=ALU.mult, op1=ALU.add).then_inc(conv_sum, 1)

            def finish_block(H):
                dve.wait_ge(skip_ready[H], 1)
                for n in range(NB):
                    dve.wait_ge(fc2_done[H], n + 1)
                    dve.tensor_tensor(X[:, H, cols(n)], big(H)[:, n, :], skip[:, H, cols(n)],
                                      ALU.add).then_inc(X_ready[H], 1)

            def keys(H):
                for n in range(NB):
                    dve.wait_ge(k_proj[H], n + 1)
                    for g in range(2):
                        ins = dve.tensor_scalar(k_split(H)[:, g, cols(n)], conv_banks(H)[:, n, :],
                                                c3("bk"), c3("minus_own")[:, g:g + 1], ALU.add, ALU.mult)
                    ins.then_inc(k_low_ready[H], 1)

            def values(H):
                dve.wait_ge(v_proj[H], 1)
                dve.tensor_tensor(v_tok[:, H * BH:(H + 1) * BH, :, :, :].rearrange("p b j g c -> p (b j) (g c)"),
                                  ps[:, 0:NB, :].rearrange("p n (t c) -> p (n t) c", c=P),
                                  c3("bv").unsqueeze(1).to_broadcast([P, 2 * BH, P]), ALU.add
                                  ).then_inc(v_ready[H], 1)

            def minima(H, u):
                unit = UNITS * H + u
                dve.wait_ge(scores_done, unit + 1)
                dve.tensor_reduce(smin[:, unit, :],
                                  ps[:, score_bank(H, u), :].rearrange("p (t i) -> p t i", t=2),
                                  AX_X, ALU.min).then_inc(min_ready, 1)

            def scale_values(H, b):
                beta = BH * H + b
                dve.wait_ge(exp_done, G * (beta + 1))
                dve.wait_ge(v_ready[H], 1)
                link(dve.reciprocal(inv_row[:, beta, :, :], psum_row[:, beta, :, :]))
                v = v_tok[:, beta, :, :, :].rearrange("p j g c -> p (j g) c")
                dve.tensor_tensor(v, v, inv_row[:, beta, :, :].rearrange("p j g -> p (j g)").unsqueeze(2)
                                  .to_broadcast([P, 2 * G, C]), ALU.mult).then_inc(v_scaled, 1)

            def finish(H, b):
                beta = BH * H + b
                dve.wait_ge(av_done, beta + 1)
                dve.tensor_tensor(y_out[:, beta, :], ps[:, av_bank(H, b), 0:NPIX],
                                  X[:, H, b * NPIX:(b + 1) * NPIX], ALU.add).then_inc(y_ready, 1)

            def normalise_input(H):
                dve.wait_ge(first_loaded, 16)
                for n in range(NB):
                    dve.wait_ge(x_loaded[H][n], 16)
                    dve.wait_ge(rstd_ready[H], n + 1)
                    dve.scalar_tensor_tensor(out=tap_view(H, CENTRE, n), in0=rows(x[:, H, cols(n)]),
                                             scalar=c1("ln1_w"), in1=rows(rstd(H)[:, cols(n)]),
                                             op0=ALU.mult, op1=ALU.mult).then_inc(normed[H], 1)

            normalise_input(0)
            dve.wait_ge(second_loaded, 16)
            dve.wait_ge(attn_border_zeroed, 3)
            attn_taps(0, range(0, 2))
            normalise_input(1)
            attn_taps(0, range(2, ATTN_DVE_TAPS))
            dve.wait_ge(kf_zeroed, 1)
            pool_keys(0)
            attn_taps(1, range(0, 1))
            softmax_in(0)
            attn_taps(1, range(1, 2))
            dve.wait_ge(blocks_zeroed, 1)
            softmax_out(0)
            attn_taps(1, range(2, 3))
            mix_weights(0)
            add_pe_taps(0)
            pool_keys(1)
            attn_taps(1, range(3, 5))
            residual(0)
            attn_taps(1, range(5, ATTN_DVE_TAPS))
            softmax_in(1)
            softmax_out(1)
            add_pe_taps(1)
            mix_weights(1)
            normalise(0)
            residual(1)
            dve.wait_ge(third_loaded, 16)
            dve.wait_ge(mlp_border_zeroed, 3)
            dve.tensor_scalar(k_bias[:, :], c3("minus_own"), c3("bk"), None, ALU.mult).then_inc(k_bias_ready, 1)
            conv_taps(0, DVE_AT["m1"])
            normalise(1)
            conv_taps(DVE_AT["m1"], DVE_AT["X0"])
            finish_block(0)
            conv_taps(DVE_AT["X0"], DVE_AT["keys0"])
            keys(0)
            conv_taps(DVE_AT["keys0"], DVE_AT["values0"])
            values(0)
            at = DVE_AT["values0"]
            for u in range(UNITS - G):
                minima(0, u)
                if u >= 5 and u % G == 1:
                    scale_values(0, u // G - 1)
                if u >= 8 and u % G == 0:
                    finish(0, u // G - 2)
                conv_taps(at, at + TAPS_AFTER_UNIT[u])
                at += TAPS_AFTER_UNIT[u]
            conv_taps(at, len(TAP_ORDER))
            for u in range(UNITS - G, UNITS - 1):
                minima(0, u)
            scale_values(0, BH - 2)
            finish(0, BH - 3)
            finish_block(1)
            minima(0, UNITS - 1)
            keys(1)
            finish(0, BH - 2)
            values(1)
            scale_values(0, BH - 1)
            for u in range(UNITS):
                minima(1, u)
                if u == 2:
                    finish(0, BH - 1)
                if u >= 6 and u % G == 2:
                    scale_values(1, (u - 6) // G)
                if u >= 11 and u % G == 3:
                    finish(1, (u - 11) // G)
            scale_values(1, BH - 1)
            finish(1, BH - 2)
            finish(1, BH - 1)


def kernel(x, L0_conv_ln1_w, L0_conv_ln2_w, L0_conv_dw_w, L0_conv_dw_b, L0_conv_qkvl_w, L0_conv_qkvl_b,
           L0_conv_fc1_w, L0_conv_fc1_b, L0_conv_pos_w, L0_conv_pos_b, L0_conv_fc2_w, L0_conv_fc2_b,
           L1_conv_Wq, L1_conv_bq, L1_conv_Wk, L1_conv_bk, L1_conv_Wv, L1_conv_bv):
    import numpy as np
    import concourse.bacc as bacc
    from concourse.bass_utils import run_bass_kernel_spmd

    f = np.float32

    def arr(a):
        return np.asarray(a)

    def tiled(a):
        return np.tile(arr(a).reshape(-1, 1), (G, 1))

    def blocks(w):
        w = arr(w)
        out = np.zeros((P, P), f)
        for g in range(G):
            out[C * g:C * (g + 1), C * g:C * (g + 1)] = w
        return out

    def diagonal(v):
        out = np.zeros((len(v), len(v)), f)
        out[np.arange(len(v)), np.arange(len(v))] = v
        return out

    slot = np.arange(P) % C
    centre = blocks(np.eye(C, dtype=f) - f(1) / f(C))
    ident = np.eye(P, dtype=f)
    mean = blocks(np.full((C, C), f(1) / f(C)))
    side2 = SIDE // 2
    pool = np.zeros((P, CLASSES, P), f)
    for cl in range(CLASSES):
        for half in range(2):
            for i in range(side2):
                for j in range(side2):
                    for a in ((i,) if cl // 2 == 0 else (i - 1, i)):
                        for b in ((j,) if cl % 2 == 0 else (j - 1, j)):
                            if a >= 0 and b >= 0:
                                pool[half * POOLED + a * side2 + b, cl, half * POOLED + i * side2 + j] = 1
    keep = diagonal((slot < C - C4).astype(f))
    is_v = (slot >= C - C4).astype(f).reshape(P, 1)
    minus_own = np.where(np.arange(P)[:, None] // C == np.arange(G)[None, :], f(-1), f(0)).astype(f)
    ones = np.zeros((P, P), f)
    ones[0] = 1

    dw = arr(L0_conv_dw_w).reshape(C2, 9)
    wall = arr(L0_conv_qkvl_w).reshape(4, C4, C2)
    ball = arr(L0_conv_qkvl_b).reshape(4, C4)
    taps = []
    for tap in ATTN_TAP_ORDER[:ATTN_PE_TAPS]:
        w = np.zeros((C, C), f)
        w[:C2, :C2] = diagonal(dw[:, tap])
        if tap == CENTRE:
            w[C2:, C2:C2 + C4] = wall[3].T
            w[C2:, C2 + C4:] = wall[2].T
        taps.append(blocks(w))
    attn_w = np.zeros((C, 9), f)
    attn_w[:C2] = dw
    attn_b = np.concatenate([arr(L0_conv_dw_b), ball[3], ball[2]])
    qk_w = np.zeros((P, 2, G, C4), f)
    qk_brow = np.zeros((P, 2, G, C4), f)
    for g in range(G):
        for which in range(2):
            qk_w[C * g + C2:C * (g + 1), which, g] = wall[which].T
            qk_brow[0, which, g] = ball[which]

    fc1 = arr(L0_conv_fc1_w).reshape(HID, C).T
    fc1_w = np.zeros((P, G, HID), f)
    for g in range(G):
        fc1_w[C * g:C * (g + 1), g] = fc1
    pos = arr(L0_conv_pos_w).reshape(HID, 9)

    def side_by_side(cols, n, **parts):
        out = np.zeros((P, n), f)
        for name, (a, b) in cols.items():
            out[:, a:b] = parts[name].reshape(P, b - a)
        return out

    first = side_by_side(FIRST_COLS, FIRST_N, centre=centre, ident=ident, mean=mean,
                         ln1_w=tiled(L0_conv_ln1_w), ln2_w=tiled(L0_conv_ln2_w))
    second = side_by_side(SECOND_COLS, SECOND_N, attn_taps=np.concatenate(taps, 1), attn_w=np.tile(attn_w, (G, 1)),
                          attn_b=tiled(attn_b), qk_w=qk_w, qk_brow=qk_brow, ones=ones, pool=pool, keep=keep,
                          is_v=is_v)
    third = side_by_side(THIRD_COLS, THIRD_N, fc1_w=fc1_w, fc1_b=arr(L0_conv_fc1_b),
                         mlp_taps=np.concatenate([diagonal(pos[:, t]) for t in range(9)], 1), pos_w=pos,
                         pos_b=arr(L0_conv_pos_b), fc2_w=arr(L0_conv_fc2_w).reshape(C, HID).T,
                         fc2_b=tiled(L0_conv_fc2_b), wq=blocks(arr(L1_conv_Wq).T), wk=blocks(arr(L1_conv_Wk).T),
                         wv=blocks(arr(L1_conv_Wv).T), bq=tiled(L1_conv_bq), bk=tiled(L1_conv_bk),
                         bv=np.broadcast_to(np.tile(arr(L1_conv_bv), G), (P, P)),
                         minus_own=minus_own)
    xs = arr(x).reshape(G, HALVES, BH, C, SIDE, SIDE).transpose(0, 3, 1, 4, 2, 5).reshape(P, HALVES * COLS)

    nc = bacc.Bacc("TRN2", target_bir_lowering=False, num_devices=1)
    arrays = {"x_in": np.ascontiguousarray(xs), "first_in": first, "second_in": second, "third_in": third}
    args = [nc.dram_tensor(n, a.shape, F32, kind="ExternalInput").ap() for n, a in arrays.items()]
    args.append(nc.dram_tensor("y", (P, HALVES * COLS), F32, kind="ExternalOutput").ap())
    build(nc, *args)
    r = run_bass_kernel_spmd(nc, [arrays], core_ids=[0])
    y = np.asarray(r.results[0]["y"]).reshape(G, C, HALVES, BH, SIDE, SIDE)
    return y.transpose(0, 2, 3, 1, 4, 5).reshape(B, C, SIDE, SIDE)
```
